# Optimizing a Trainium2 kernel written in Bass

```python
import numpy as np
import jax
import jax.numpy as jnp

def _softmax(x, axis=-1):
    return jax.nn.softmax(x, axis=axis)

def _gelu(x):
    return jax.nn.gelu(x, approximate=True)

def _silu(x):
    return jax.nn.silu(x)

def _sigmoid(x):
    return jax.nn.sigmoid(x)

def _layernorm(x, axis=-1, eps=1e-05):
    m = jnp.mean(x, axis=axis, keepdims=True)
    v = jnp.var(x, axis=axis, keepdims=True)
    return (x - m) / jnp.sqrt(v + eps)

def _scatter_add(tgt, idx, src, axis=0):
    return tgt.at[idx].add(src)

def _segment_sum(src, seg, n):
    return jax.ops.segment_sum(src, seg, n)
kernel_name = 'mk_gnn_preln_d2_gnn_r8_421809'

def setup_inputs(seed: int=0):
    np.random.seed(seed)
    _w = jnp.asarray

    def _rec_inputs():
        import jax
        import jax.numpy as jnp
        _gk = jax.random.key(seed)
        x = -0.0002117 + 1 * jax.random.normal(jax.random.fold_in(_gk, 1), (6250, 256), jnp.float32)
        src = jax.random.randint(jax.random.fold_in(_gk, 2), (200000,), 0, 6250, jnp.int32)
        dst = jax.random.randint(jax.random.fold_in(_gk, 3), (200000,), 0, 6250, jnp.int32)
        _o = jnp.argsort(dst, stable=True)
        src = src[_o]
        dst = dst[_o]
        return (x, src, dst)
    x, src, dst = _rec_inputs()

    def _L0_gnn_setup():
        import jax, jax.numpy as jnp
        import numpy as np
        N_NODES = 12500
        N_EDGES = 400000
        IN_F = 256
        OUT_F = 256
        NEG_SLOPE = 0.2
        key = jax.random.key(seed)
        ks = jax.random.split(key, 8)
        x = jax.random.normal(ks[0], (N_NODES, IN_F), dtype=jnp.float32)
        Wv = jax.random.normal(ks[1], (IN_F, OUT_F), dtype=jnp.float32) / np.sqrt(IN_F)
        bv = jnp.zeros((OUT_F,), dtype=jnp.float32)
        wq = jax.random.normal(ks[2], (OUT_F,), dtype=jnp.float32) / np.sqrt(OUT_F)
        bq = jnp.zeros((), dtype=jnp.float32)
        wk = jax.random.normal(ks[3], (OUT_F,), dtype=jnp.float32) / np.sqrt(OUT_F)
        bk = jnp.zeros((), dtype=jnp.float32)
        src = jax.random.randint(ks[4], (N_EDGES,), 0, N_NODES, dtype=jnp.int32)
        dst = jax.random.randint(ks[5], (N_EDGES,), 0, N_NODES, dtype=jnp.int32)
        return {'x': x, 'Wv': Wv, 'bv': bv, 'wq': wq, 'bq': bq, 'wk': wk, 'bk': bk, 'src': src, 'dst': dst}
    _L0_gnn_all = _L0_gnn_setup()
    _L0_gnn_in = {k: v for k, v in _L0_gnn_all.items() if k in ('Wv', 'bv', 'wq', 'bq', 'wk', 'bk')}
    del _L0_gnn_all

    def _L1_gnn_setup():
        import jax, jax.numpy as jnp
        import numpy as np
        N_NODES = 3125
        N_EDGES = 50000
        D = 256
        key = jax.random.key(seed)
        k1, k2, k3, k4, k5 = jax.random.split(key, 5)
        feat = jax.random.normal(k1, (N_NODES, D), dtype=jnp.float32)
        src = jax.random.randint(k2, (N_EDGES,), 0, N_NODES, dtype=jnp.int32)
        dst = jax.random.randint(k3, (N_EDGES,), 0, N_NODES, dtype=jnp.int32)
        a = float(np.sqrt(6.0 / (D + D)))
        W1 = jax.random.uniform(k4, (D, D), minval=-a, maxval=a, dtype=jnp.float32)
        W2 = jax.random.uniform(k5, (D, D), minval=-a, maxval=a, dtype=jnp.float32)
        b = jnp.zeros((D,), dtype=jnp.float32)
        return {'feat': feat, 'W1': W1, 'W2': W2, 'b': b, 'src': src, 'dst': dst}
    _L1_gnn_all = _L1_gnn_setup()
    _L1_gnn_in = {k: v for k, v in _L1_gnn_all.items() if k in ('W1', 'W2', 'b')}
    del _L1_gnn_all
    return {'x': x, 'src': src, 'dst': dst, 'L0_gnn_Wv': _L0_gnn_in['Wv'], 'L0_gnn_bv': _L0_gnn_in['bv'], 'L0_gnn_wq': _L0_gnn_in['wq'], 'L0_gnn_bq': _L0_gnn_in['bq'], 'L0_gnn_wk': _L0_gnn_in['wk'], 'L0_gnn_bk': _L0_gnn_in['bk'], 'L1_gnn_W1': _L1_gnn_in['W1'], 'L1_gnn_W2': _L1_gnn_in['W2'], 'L1_gnn_b': _L1_gnn_in['b']}

def reference(x, src, dst, L0_gnn_Wv, L0_gnn_bv, L0_gnn_wq, L0_gnn_bq, L0_gnn_wk, L0_gnn_bk, L1_gnn_W1, L1_gnn_W2, L1_gnn_b):
    import jax
    import jax.numpy as jnp

    def _L0_gnn_ref(x, Wv, bv, wq, bq, wk, bk, src, dst):
        import jax, jax.numpy as jnp
        import numpy as np
        N_NODES = 12500
        N_EDGES = 400000
        IN_F = 256
        OUT_F = 256
        NEG_SLOPE = 0.2
        n = x.shape[0]
        h = x @ Wv + bv
        q = h @ wq + bq
        k = h @ wk + bk
        e = q[src] + k[dst]
        c = jnp.where(e > 0, e, NEG_SLOPE * e)
        m = jax.ops.segment_max(c, dst, num_segments=n)
        ex = jnp.exp(c - m[dst])
        s = jax.ops.segment_sum(ex, dst, num_segments=n)
        attn = ex / s[dst]
        msg = h[src] * attn[:, None]
        out = jax.ops.segment_sum(msg, dst, num_segments=n)
        return out

    def _L1_gnn_ref(feat, W1, W2, b, src, dst):
        import jax, jax.numpy as jnp
        import numpy as np
        N_NODES = 3125
        N_EDGES = 50000
        D = 256
        n = feat.shape[0]
        ones = jnp.ones(src.shape[0], dtype=feat.dtype)
        out_deg = jnp.maximum(jax.ops.segment_sum(ones, src, num_segments=n), 1.0)
        in_cnt = jax.ops.segment_sum(ones, dst, num_segments=n)
        t1 = feat @ W1
        msg = t1[src] + feat[src] * feat[dst] @ W2
        scale = jnp.sqrt(out_deg[src]) * jnp.sqrt(out_deg[dst])
        msg = msg / scale[:, None]
        agg = jax.ops.segment_sum(msg, dst, num_segments=n)
        embed = jnp.where(in_cnt[:, None] > 0, t1 + agg, jnp.zeros_like(t1))
        embed = embed + b
        embed = jax.nn.leaky_relu(embed, negative_slope=0.01)
        norm = jnp.linalg.norm(embed, axis=1, keepdims=True)
        embed = embed / jnp.maximum(norm, 1e-12)
        return embed
    h = jnp.maximum(_layernorm(x, axis=-1), 0.0)
    x = x + _L0_gnn_ref(h, L0_gnn_Wv, L0_gnn_bv, L0_gnn_wq, L0_gnn_bq, L0_gnn_wk, L0_gnn_bk, src, dst)
    h = jnp.maximum(_layernorm(x, axis=-1), 0.0)
    x = x + _L1_gnn_ref(h, L1_gnn_W1, L1_gnn_W2, L1_gnn_b, src, dst)
    return x

_drawn_inputs = setup_inputs


def setup_inputs(seed=0):
    import zlib

    import numpy as np

    out = dict(_drawn_inputs(seed))
    spreads = {'L0_gnn_bv': (0.0, 0.1), 'L1_gnn_b': (0.0, 2.0)}
    factors = {'L0_gnn_wk': 2.81, 'L1_gnn_W2': 2.819}
    for name, (base, spread) in spreads.items():
        noise = np.random.default_rng([zlib.crc32(name.encode()), seed]).standard_normal(out[name].shape)
        drawn = base * np.exp(spread * noise) if base else spread * noise
        out[name] = jnp.asarray(drawn.astype(out[name].dtype))
    for name, factor in factors.items():
        out[name] = (out[name] * factor).astype(out[name].dtype)
    return out
```

```python
import concourse.bass as bass
from concourse import mybir
from contextlib import ExitStack

N, D, E = 6250, 256, 200000
P = 125
NB = N // P
T = 34
TC = T // 2
WIN = T * 128
RMAX = -(-E // WIN)
TW = 264
ONE, QC, RS = D, D + 1, D
EC = E // P
SPL = 160
NS = E // SPL
HT = EC // NB
BIG = 1e28
NODST = 7000.0
UP = 1
MAGIC = 12582912.0


def gnn(nc, x, src, dst, Wv, bv, wq, bq, wk, bk, W1, W2, b1, out):
    f32, bf16, i32, u32, u8 = mybir.dt.float32, mybir.dt.bfloat16, mybir.dt.int32, mybir.dt.uint32, mybir.dt.uint8
    ALU, ACT, AX = mybir.AluOpType, mybir.ActivationFunctionType, mybir.AxisListType

    edges = nc.dram_tensor("edges", (E + WIN, 2), i32).ap()
    splits = nc.dram_tensor("splits", (NS,), f32).ap()
    startd = nc.dram_tensor("startd", (NB + 1,), f32).ap()
    wind = nc.dram_tensor("wind", (1, RMAX * NB), i32).ap()
    tab0 = nc.dram_tensor("tab0", (N, TW), f32).ap()
    tab1 = nc.dram_tensor("tab1", (N, TW), f32).ap()
    x1d = nc.dram_tensor("x1d", (N, D), f32).ap()

    ctx = ExitStack()
    with ctx:
        def sb(name, shape, dt=f32):
            return ctx.enter_context(nc.sbuf_tensor(name, shape, dt))

        def pb(name, shape, dt=f32):
            return ctx.enter_context(nc.psum_tensor(name, shape, dt))

        def sem(name):
            return ctx.enter_context(nc.semaphore(name))

        rows = [sb(f"rows{h}", [128, T, TW]) for h in range(2)]
        wts = [sb(f"wts{h}", [128, T, P]) for h in range(2)]
        acc = sb("acc", [P, NB, D + 1])
        edge = [sb(f"edge{h}", [128, T, 2], i32) for h in range(2)]
        ndl = [sb(f"ndl{h}", [128, T]) for h in range(2)]
        oh_lo_m = sb("oh_lo_m", [P, HT * P], bf16)
        oh_lo = oh_lo_m[:].rearrange("p (t s) -> p t s", s=P)
        oh_hi = sb("oh_hi", [P, HT, NB], bf16)
        src_lo = sb("src_lo", [P, EC], u8)
        src_hi = sb("src_hi", [P, EC], u8)
        slot_i = sb("slot_i", [128, 128], i32)
        slot = sb("slot", [128, 128])
        slot_b = sb("slot_b", [128, 128], bf16)
        part_i = sb("part_i", [128, 1], i32)
        part = sb("part", [128, 1])
        ident = sb("ident", [128, 128])
        ones = sb("ones", [128, 128])
        base_i = sb("base_i", [128, NB], i32)
        base = sb("base", [128, NB])
        thr = sb("thr", [128, 1])
        first = sb("first", [128, RMAX + 1])
        later = sb("later", [128, RMAX + 1])
        rstep_i = sb("rstep_i", [1, RMAX + 1], i32)
        rstep = sb("rstep", [1, RMAX + 1])
        Wv_s = sb("Wv_s", [128, 2, D])
        W1_s = sb("W1_s", [128, 2, D])
        W2_s = sb("W2_s", [128, 2, D])
        bv_s, wq_s, wk_s, b1_s = (sb(n, [P, D]) for n in ("bv_s", "wq_s", "wk_s", "b1_s"))
        primed = sb("primed", [1, 8])
        bqk = sb("bqk", [P, 2])
        mv = sb("mv", [P, NB, 2])
        rstd = sb("rstd", [P, NB])
        nmr = sb("nmr", [P, NB])
        rstd1 = sb("rstd1", [P, NB])
        nmr1 = sb("nmr1", [P, NB])
        kcol = sb("kcol", [P, NB])
        mcol = sb("mcol", [P, NB])
        outdeg = sb("outdeg", [P, NB])
        sod = sb("sod", [P, NB])
        rso = sb("rso", [P, NB])
        filled = sb("filled", [P, NB])
        stats = sb("stats", [P, NB, 6])
        hn = [sb(f"hn{h}", [P, D]) for h in range(2)]
        hT = [sb(f"hT{h}", [128, 4, P]) for h in range(2)]
        trow = [sb(f"trow{h}", [P, TW]) for h in range(2)]
        junk = sb("junk", [P, D])
        xt = [sb(f"xt{h}", [P, D]) for h in range(2)]
        x1t = [sb(f"x1t{h}", [P, D]) for h in range(2)]
        U, F = x1t, hn
        y = [sb(f"y{h}", [P, D]) for h in range(2)]
        qm = sb("qm", [128, 3, P])
        dk = sb("dk", [P, P])
        dm = sb("dm", [P, P])
        sm = sb("sm", [P, 12])
        spl_s = sb("spl_s", [P, EC // SPL])
        cnt = sb("cnt", [NB + 1, 6])
        chunk = sb("chunk", [NB + 1, SPL], i32)
        chunk_f = sb("chunk_f", [NB + 1, SPL])
        chunk_i = sb("chunk_i", [NB + 1, 1], u32)
        st_row = sb("st_row", [1, NB + 1])
        gap = sb("gap", [1, NB])
        rnd_f = sb("rnd_f", [1, RMAX + 4])
        rnd = sb("rnd", [1, 1], i32)
        padi = sb("padi", [128, T, 2], i32)

        win = wts[1][0:1, :, :].rearrange("p a b -> p (a b)")[:, 0:RMAX * NB].bitcast(i32)
        spl_b = oh_lo_m[0:NB + 1, 0:2 * NS].bitcast(f32)
        srcs = wts[0][0:P, :, :].rearrange("p a b -> p (a b)")[:, 0:EC].bitcast(i32)
        dsts = wts[0][0:P, :, :].rearrange("p a b -> p (a b)")[:, EC:2 * EC].bitcast(i32)
        pairs = wts[1][0:P, :, :].rearrange("p a b -> p (a b)")[:, 0:2 * EC].bitcast(i32) \
            .rearrange("p (e c) -> p e c", c=2)
        tmp_hi = rows[0][0:P, :, :].rearrange("p a b -> p (a b)")[:, T * TW - EC:T * TW]
        tmp_lo = rows[1][0:P, :, :].rearrange("p a b -> p (a b)")[:, T * TW - EC:T * TW]
        XH = NB // 2
        xs = [rows[h][0:P, :, :].rearrange("p a b -> p (a b)")[:, 0:XH * D]
              .rearrange("p (t d) -> p t d", d=D) for h in range(2)]

        ps_q = pb("ps_q", [128, 512])
        ps_k = pb("ps_k", [128, 512])
        ps_m = pb("ps_m", [128, 512])
        ps_h = pb("ps_h", [128, 512])
        ps_a = [pb(f"ps_a{h}", [128, 512]) for h in range(2)]
        ps_t = pb("ps_t", [128, 4, 128])
        ps_o = pb("ps_o", [128, 512])
        ps_tt = [ps_t[:], ps_o[:].rearrange("p (c n) -> p c n", n=128)]

        names = """edges_in consts_in x_in0 x_in1 xhalf iotas dve_iota pairs_made pairs_out pads_made split_made
            split_out split_in chunk_at chunk_in start_made start_out start_in windows_made windows_out lohi
            pre_std pre_rstd pre_scaled hn_made hn_T hT_made h_ps h_row pre_tab
            edge_in0 edge_in1 ndl_made0 ndl_made1 sq_made0 sq_made1 got00 got01 got10 got11
            used00 used01 used10 used11 half_max qT_made dk_made dm_made kb_made mb_made
            e_made0 e_made1 w_made00 w_made01 w_made10 w_made11 corr_in corr_made acc_made0 acc_made1
            oh_made hist_ps hist_made x_in_l0 x_in_l1 x1_made0 x1_made1 std1_in std1_made
            scaled1 f_made0 f_made1 f_out0 f_out1 x1_out0 x1_out1 deg_made sod_made rs_made rs_out
            eq_made x1_in0 x1_in1 f2_made0 f2_made1 up_made upT_made upT_copied o_ps o_read ss_made norm_made
            y_out0 y_out1 y_made0 y_made1 settled dve_c pool_c""".split()
        S = {n: sem(n) for n in names}
        counters = """used00 used01 used10 used11 ndl_made0 ndl_made1 x1_made0 x1_made1 f_made0 f_made1
            hist_ps hist_made e_made0 e_made1 y_made0 y_made1 upT_made upT_copied o_read hT_made h_row
            w_made00 w_made01 w_made10 w_made11""".split()
        stores = "x1_out0 x1_out1 f_out0 f_out1 y_out0 y_out1 pre_tab".split()

        def flat(t):
            return t.rearrange("p a b -> p (a b)")

        def over_tiles(col, n, w):
            return col.unsqueeze(1).to_broadcast([col.shape[0], n, w])

        def over_slots(col, n, w):
            return col.unsqueeze(2).to_broadcast([col.shape[0], n, w])

        def settle(eng):
            eng.sem_inc(S["settled"], 1)

        def rounds(eng):
            return eng.value_load(rnd[0:1, 0:1], min_val=1, max_val=RMAX)

        block = ctx.enter_context(nc.Block())

        @block.sync
        def _(sp):
            sp.dma_start(dsts, dst.rearrange("(p e) -> p e", p=P)).then_inc(S["edges_in"], 16)
            sp.dma_start(srcs, src.rearrange("(p e) -> p e", p=P)).then_inc(S["edges_in"], 16)
            xv = x.rearrange("(t p) d -> p t d", p=P)
            for h in range(2):
                sp.dma_start(xs[h], xv[:, h * XH:(h + 1) * XH, :]).then_inc(S[f"x_in{h}"], 16)
            sp.wait_ge(S["split_made"], 1)
            sp.dma_start(splits.rearrange("(p s) -> p s", p=P), spl_s[:]).then_inc(S["split_out"], 16)
            sp.wait_ge(S["split_out"], 16)
            sp.dma_start(spl_b, splits.unsqueeze(0).to_broadcast([NB + 1, NS])).then_inc(S["split_in"], 16)
            sp.wait_ge(S["pairs_made"], 1)
            sp.dma_start(edges[0:E, :].rearrange("(p e) c -> p e c", p=P), pairs).then_inc(S["pairs_out"], 16)
            sp.wait_ge(S["pads_made"], 1)
            sp.dma_start(edges[E:E + WIN, :].rearrange("(p e) c -> p e c", p=128), padi[:]).then_inc(S["pairs_out"], 16)
            sp.wait_ge(S["start_made"], 1)
            sp.dma_start(startd.unsqueeze(1), cnt[:, 4:5]).then_inc(S["start_out"], 16)
            sp.wait_ge(S["start_out"], 16)
            sp.dma_start(st_row[:], startd.unsqueeze(0)).then_inc(S["start_in"], 16)
            sp.wait_ge(S["pairs_out"], 32)
            sp.wait_ge(S["windows_made"], 1)
            sp.dma_start(wind, win).then_inc(S["windows_out"], 16)
            with sp.Fori(0, XH) as p:
                for h in range(2):
                    sp.wait_ge(S["h_row"], UP + 2 * p + h + 1)
                    sp.dma_start(tab0[bass.ds((2 * p + h) * P, P), :], trow[h][:]).then_inc(S["pre_tab"], 16)
            sp.wait_ge(S["windows_out"], 16)
            R = rounds(sp)
            sp.wait_ge(S["pre_tab"], 16 + 16 * NB)
            with sp.Fori(0, R) as r:
                with sp.Fori(0, XH) as p:
                    k = r * XH + p
                    for h in range(2):
                        e0 = sp.value_load(wind[0:1, bass.ds(r * NB + 2 * p + h, 1)], min_val=0, max_val=E)
                        sp.wait_ge(S[f"w_made{h}1"], UP + k)
                        sp.dma_start(edge[h][:], edges[bass.ds(e0, WIN), :].rearrange("(p e) c -> p e c", p=128)) \
                            .then_inc(S[f"edge_in{h}"], 16)
                        sp.wait_ge(S[f"x1_made{h}"], UP + k)
                        sp.dma_start(xt[h][:], x[bass.ds((2 * p + h) * P, P), :]).then_inc(S[f"x_in_l{h}"], 16)
            KR = R * XH
            for h in range(2):
                sp.wait_ge(S[f"x1_out{h}"], 16 + KR * 16)
            sp.wait_ge(S["f_out0"], 16 + KR * 16)
            sp.wait_ge(S["f_out1"], 16 + KR * 16)
            sp.wait_ge(S["rs_made"], 1)
            with nc.allow_non_contiguous_dma(reason="one column of the table"):
                sp.dma_start(tab1.rearrange("(t p) c -> p t c", p=P)[:, :, RS:RS + 1], rso[:].unsqueeze(2)) \
                    .then_inc(S["rs_out"], 16)
            with sp.Fori(0, R) as r:
                with sp.Fori(0, XH) as p:
                    k = r * XH + p + KR
                    for h in range(2):
                        e0 = sp.value_load(wind[0:1, bass.ds(r * NB + 2 * p + h, 1)], min_val=0, max_val=E)
                        sp.wait_ge(S[f"w_made{h}1"], UP + k)
                        sp.dma_start(edge[h][:], edges[bass.ds(e0, WIN), :].rearrange("(p e) c -> p e c", p=128)) \
                            .then_inc(S[f"edge_in{h}"], 16)
                        sp.wait_ge(S[f"y_made{h}"], UP + r * XH + p)
                        sp.dma_start(xt[h][:], x1d[bass.ds((2 * p + h) * P, P), :]).then_inc(S[f"x1_in{h}"], 16)
            for h in range(2):
                sp.wait_ge(S[f"y_out{h}"], 16 + KR * 16)
            settle(sp)

        @block.gpsimd
        def _(pool):
            nc.gpsimd.iota(slot_i[:], [[1, 128]], base=0, channel_multiplier=0).then_inc(S["iotas"], 1)
            nc.gpsimd.iota(part_i[:], [[0, 1]], base=0, channel_multiplier=1).then_inc(S["iotas"], 1)
            nc.gpsimd.iota(base_i[:], [[P, NB]], base=0, channel_multiplier=0).then_inc(S["iotas"], 1)
            nc.gpsimd.iota(rstep_i[:], [[WIN, RMAX + 1]], base=0, channel_multiplier=0).then_inc(S["iotas"], 1)
            nc.gpsimd.memset(ones[:], 1.0).then_inc(S["iotas"], 1)
            nc.gpsimd.memset(later[:, 0:1], 0.0).then_inc(S["iotas"], 1)
            nc.gpsimd.memset(later[:, 1:RMAX + 1], 1.0).then_inc(S["iotas"], 1)
            nc.gpsimd.memset(first[:, 0:1], 1.0).then_inc(S["iotas"], 1)
            nc.gpsimd.memset(first[:, 1:RMAX + 1], 0.0).then_inc(S["iotas"], 1)
            nc.gpsimd.memset(outdeg[:], 0.0).then_inc(S["iotas"], 1)
            nc.gpsimd.memset(mcol[:], -1e30).then_inc(S["iotas"], 1)
            for h in range(2):
                nc.gpsimd.memset(trow[h][:, D:TW], 0.0).then_inc(S["pool_c"], 1)
                pool.wait_ge(S["pool_c"], h + 1)
                nc.gpsimd.memset(trow[h][:, ONE:ONE + 1], 1.0).then_inc(S["iotas"], 1)
            nc.gpsimd.memset(padi[:, :, 0:1], 0).then_inc(S["pool_c"], 1)
            nc.gpsimd.memset(padi[:, :, 1:2].bitcast(f32), NODST).then_inc(S["pool_c"], 1)
            pool.wait_ge(S["pool_c"], 4)
            pool.sem_inc(S["pads_made"], 1)
            nc.gpsimd.memset(acc[:], 0.0).then_inc(S["iotas"], 1)
            pool.wait_ge(S["edges_in"], 32)
            nc.gpsimd.tensor_scalar(tmp_hi, srcs, 0.5, 1.0 / P, ALU.add, ALU.mult).then_inc(S["pool_c"], 1)
            pool.wait_ge(S["pool_c"], 5)
            nc.gpsimd.tensor_scalar(tmp_hi, tmp_hi, -0.5, None, ALU.add).then_inc(S["pool_c"], 1)
            pool.wait_ge(S["pool_c"], 6)
            nc.gpsimd.tensor_scalar(tmp_hi, tmp_hi, MAGIC, None, ALU.add).then_inc(S["pool_c"], 1)
            pool.wait_ge(S["pool_c"], 7)
            nc.gpsimd.tensor_scalar(tmp_hi, tmp_hi, -MAGIC, None, ALU.add).then_inc(S["pool_c"], 1)
            pool.wait_ge(S["pool_c"], 8)
            nc.gpsimd.tensor_copy(src_hi[:], tmp_hi).then_inc(S["lohi"], 1)
            nc.gpsimd.tensor_scalar(tmp_lo, tmp_hi, -float(P), None, ALU.mult).then_inc(S["lohi"], 1)
            pool.wait_ge(S["chunk_at"], 1)
            nc.gpsimd.indirect_dma_start(chunk[:], None, dst.rearrange("(a b) -> a b", b=1),
                                         bass.IndirectOffsetOnAxis(chunk_i[:], 0)).then_inc(S["chunk_in"], 16)
            pool.wait_ge(S["lohi"], 3)
            pool.wait_ge(S["pre_tab"], 16 + 16 * NB)
            pool.wait_ge(S["windows_made"], 1)
            R = rounds(pool)
            for layer in range(2):
                table = (tab0, tab1)[layer]
                if layer:
                    pool.wait_ge(S["rs_out"], 16)
                with pool.Fori(0, R) as r:
                    with pool.Fori(0, XH) as p:
                        k = r * XH + p + (R * XH if layer else 0)
                        for h in range(2):
                            pool.wait_ge(S[f"edge_in{h}"], 16 * (k + 1))
                            for c in range(2):
                                pool.wait_ge(S[f"used{h}{c}"], UP + k)
                                settle(pool)
                                for t in range(c * TC, (c + 1) * TC):
                                    nc.gpsimd.indirect_dma_start(
                                        rows[h][:, t, :], None, table,
                                        bass.IndirectOffsetOnAxis(edge[h][:, t, 0:1].bitcast(u32), 0)) \
                                        .then_inc(S[f"got{h}{c}"], 16)

        @block.vector
        def _(dve):
            V = nc.vector
            made = [0, 0]

            def own(ins):
                made[0] += 1
                ins.then_inc(S["dve_c"], 1)
                dve.wait_ge(S["dve_c"], made[1] + made[0])

            dve.wait_ge(S["edges_in"], 32)
            own(V.tensor_copy(pairs[:, :, 1:2].bitcast(f32), dsts.unsqueeze(2)))
            V.tensor_copy(spl_s[:], pairs[:, 0:EC:SPL, 1:2].bitcast(f32).rearrange("p e c -> p (e c)")).then_inc(S["split_made"], 1)
            V.tensor_copy(pairs[:, :, 0:1], srcs.unsqueeze(2)).then_inc(S["pairs_made"], 1)
            dve.wait_ge(S["iotas"], 14)
            own(V.tensor_copy(slot[:], slot_i[:]))
            own(V.tensor_copy(slot_b[:], slot_i[:]))
            own(V.tensor_copy(part[:], part_i[:]))
            own(V.tensor_copy(base[:], base_i[:]))
            own(V.tensor_copy(rstep[:], rstep_i[:]))
            V.tensor_scalar(ident[:], slot[:], part[:, 0:1], None, ALU.is_equal).then_inc(S["dve_iota"], 1)
            own(V.tensor_scalar(thr[:], part[:], float(P), None, ALU.mult))
            dve.wait_ge(S["split_in"], 16)
            own(V.tensor_scalar(spl_b, spl_b, thr[0:NB + 1, 0:1], None, ALU.is_lt))
            own(V.tensor_reduce(cnt[:, 0:1], spl_b, AX.X, ALU.add))
            own(V.tensor_scalar(cnt[:, 1:2], cnt[:, 0:1], -1.0, 0.0, ALU.add, ALU.max))
            own(V.tensor_scalar(cnt[:, 2:3], cnt[:, 1:2], float(SPL), None, ALU.mult))
            V.tensor_copy(chunk_i[:], cnt[:, 2:3]).then_inc(S["chunk_at"], 1)
            for h in range(2):
                dve.wait_ge(S[f"x_in{h}"], 16)
                for t in range(XH):
                    last = V.bn_stats(stats[:, h * XH + t, :], xs[h][:, t, :])
                own(last)
            for t in range(NB):
                last = V.bn_aggr(mv[:, t, :], stats[:, t, :])
            own(last)
            own(V.tensor_scalar(nmr[:].unsqueeze(2), mv[:, :, 1:2], 1e-5, None, ALU.add))
            V.tensor_scalar(nmr[:], nmr[:], 1.0, None, ALU.mult).then_inc(S["pre_std"], 1)
            dve.wait_ge(S["pre_rstd"], 1)
            own(V.reciprocal(rstd[:], rstd[:]))
            own(V.tensor_tensor(nmr[:].unsqueeze(2), mv[:, :, 0:1], rstd[:].unsqueeze(2), ALU.mult))
            V.tensor_scalar(nmr[:], nmr[:], -1.0, None, ALU.mult).then_inc(S["pre_scaled"], 1)
            dve.wait_ge(S["chunk_in"], 16)
            own(V.tensor_copy(chunk_f[:], chunk[:]))
            own(V.tensor_scalar(chunk_f[:], chunk_f[:], thr[0:NB + 1, 0:1], None, ALU.is_lt))
            own(V.tensor_reduce(cnt[:, 3:4], chunk_f[:], AX.X, ALU.add))
            V.tensor_tensor(cnt[:, 4:5], cnt[:, 3:4], cnt[:, 2:3], ALU.add).then_inc(S["start_made"], 1)
            dve.wait_ge(S["lohi"], 2)
            V.tensor_tensor(src_lo[:], tmp_lo, srcs, ALU.add).then_inc(S["lohi"], 1)
            dve.wait_ge(S["start_in"], 16)
            dve.wait_ge(S["pairs_out"], 32)
            own(V.tensor_tensor(win.rearrange("p (r b) -> p r b", b=NB), over_tiles(st_row[:, 0:NB], RMAX, NB),
                                over_slots(rstep[:, 0:RMAX], RMAX, NB), ALU.add))
            own(V.tensor_scalar(win, win, float(E), None, ALU.min))
            own(V.tensor_tensor(gap[:], st_row[:, 1:NB + 1], st_row[:, 0:NB], ALU.subtract))
            own(V.tensor_reduce(rnd_f[:, 0:1], gap[:], AX.X, ALU.max))
            own(V.tensor_scalar(rnd_f[:, 2:2 + RMAX], rstep[:, 0:RMAX], rnd_f[:, 0:1], None, ALU.is_lt))
            own(V.tensor_reduce(rnd_f[:, 1:2], rnd_f[:, 2:2 + RMAX], AX.X, ALU.add))
            V.tensor_scalar(rnd[:], rnd_f[:, 1:2], 1.0, None, ALU.max).then_inc(S["windows_made"], 1)
            dve.wait_ge(S["consts_in"], 9 * 16)
            made[1], start = made[0], made[0]
            made[0] = 0
            n_own = 3
            with dve.Fori(0, XH) as p:
                for h in range(2):
                    made[0] = 0
                    made[1] = start + (2 * p + h) * n_own
                    t = 2 * p + h
                    dve.wait_ge(S["h_ps"], t + 1)
                    if h == 0:
                        dve.wait_ge(S["pre_tab"], 16 + 32 * p)
                    own(V.tensor_tensor(trow[h][:, 0:D], ps_a[h][0:P, 0:D], bv_s[:], ALU.add))
                    own(V.tensor_tensor_reduce(out=junk[:], in0=trow[h][:, 0:D], in1=wq_s[:], scale=1.0, scalar=0.0,
                                               op0=ALU.mult, op1=ALU.add, accum_out=sm[:, 0:1]))
                    own(V.tensor_tensor_reduce(out=junk[:], in0=trow[h][:, 0:D], in1=wk_s[:], scale=1.0, scalar=0.0,
                                               op0=ALU.mult, op1=ALU.add, accum_out=sm[:, 1:2]))
                    V.tensor_scalar(kcol[:, bass.ds(t, 1)], sm[:, 1:2], bqk[:, 1:2], None, ALU.add)
                    V.tensor_scalar(trow[h][:, QC:QC + 1], sm[:, 0:1], bqk[:, 0:1], None, ALU.add).then_inc(S["h_row"], 1)
                    assert made[0] == n_own
            dve.wait_ge(S["lohi"], 3)
            R = rounds(dve)
            start += NB * n_own
            n_own = 19
            with dve.Fori(0, R) as r:
                with dve.Fori(0, XH) as p:
                    k = r * XH + p
                    for h in range(2):
                        i, b = 2 * k + h, 2 * p + h
                        col = bass.ds(b, 1)
                        made[0], made[1] = 0, start + i * n_own
                        w = wts[h]
                        dve.wait_ge(S[f"edge_in{h}"], 16 * (k + 1))
                        V.tensor_scalar(ndl[h][:].unsqueeze(2), edge[h][:, :, 1:2].bitcast(f32), -1.0, base[:, col],
                                        ALU.mult, ALU.add).then_inc(S[f"ndl_made{h}"], 1)
                        V.tensor_scalar(dk[:], ident[0:P, 0:P], kcol[:, col], None, ALU.mult).then_inc(S["dk_made"], 1)
                        for c in range(2):
                            part_ = w[:, c * TC:(c + 1) * TC, :]
                            if c == 0:
                                dve.wait_ge(S[f"sq_made{h}"], k + 1)
                            dve.wait_ge(S[f"got{h}{c}"], TC * 16 * (k + 1))
                            own(V.scalar_tensor_tensor(
                                out=part_, in0=part_, scalar=-BIG,
                                in1=rows[h][:, c * TC:(c + 1) * TC, QC:QC + 1].to_broadcast([128, TC, P]),
                                op0=ALU.mult, op1=ALU.add))
                            own(V.tensor_reduce(qm[:, c, :], part_.rearrange("p t s -> p s t"), AX.X, ALU.max))
                        V.tensor_tensor(qm[:, 2, :], qm[:, 0, :], qm[:, 1, :], ALU.max).then_inc(S["half_max"], 1)
                        dve.wait_ge(S["qT_made"], i + 1)
                        own(V.tensor_reduce(sm[:, 2:3], ps_q[0:P, 0:128], AX.X, ALU.max))
                        own(V.tensor_tensor(sm[:, 3:4], sm[:, 2:3], kcol[:, col], ALU.add))
                        own(V.scalar_tensor_tensor(out=sm[:, 4:5], in0=sm[:, 3:4], scalar=0.2, in1=sm[:, 3:4],
                                                   op0=ALU.mult, op1=ALU.max))
                        own(V.tensor_tensor(sm[:, 5:6], sm[:, 4:5], mcol[:, col], ALU.max))
                        V.tensor_scalar(dm[:], ident[0:P, 0:P], sm[:, 5:6], None, ALU.mult).then_inc(S["dm_made"], 1)
                        V.tensor_tensor(sm[:, 6:7], mcol[:, col], sm[:, 5:6], ALU.subtract).then_inc(S["corr_in"], 1)
                        dve.wait_ge(S["corr_in"], i + 1)
                        own(V.tensor_tensor(mcol[:, col], sm[:, 5:6], sm[:, 5:6], ALU.max))
                        dve.wait_ge(S["kb_made"], i + 1)
                        for c in range(2):
                            part_ = w[:, c * TC:(c + 1) * TC, :]
                            own(V.tensor_tensor(part_, part_, over_tiles(ps_k[:, 0:P], TC, P), ALU.add))
                            own(V.scalar_tensor_tensor(out=part_, in0=part_, scalar=0.2, in1=part_,
                                                       op0=ALU.mult, op1=ALU.max))
                            if c == 0:
                                dve.wait_ge(S["mb_made"], i + 1)
                            V.tensor_tensor(part_, part_, over_tiles(ps_m[:, 0:P], TC, P),
                                            ALU.subtract).then_inc(S[f"e_made{c}"], 1)
                        dve.wait_ge(S["hist_ps"], UP + i)
                        cols = bass.ds(b * HT, HT)
                        V.tensor_tensor(oh_lo, over_tiles(slot_b[0:P, 0:P], HT, P),
                                        over_slots(src_lo[:, cols], HT, P), ALU.is_equal).then_inc(S["oh_made"], 1)
                        V.tensor_tensor(oh_hi[:], over_tiles(slot_b[0:P, 0:NB], HT, NB),
                                        over_slots(src_hi[:, cols], HT, NB), ALU.is_equal).then_inc(S["oh_made"], 1)
                        dve.wait_ge(S["corr_made"], i + 1)
                        dve.wait_ge(S[f"used{h}1"], UP + k + 1)
                        own(V.scalar_tensor_tensor(out=acc[:, col, :].rearrange("p a d -> p (a d)"),
                                                   in0=acc[:, col, :].rearrange("p a d -> p (a d)"),
                                                   scalar=sm[:, 7:8], in1=ps_a[h][0:P, 0:D + 1],
                                                   op0=ALU.mult, op1=ALU.add))
                        own(V.tensor_scalar(sm[:, 8:9], acc[:, col, D:D + 1].rearrange("p a d -> p (a d)"), 1e-30, None, ALU.max))
                        own(V.reciprocal(sm[:, 8:9], sm[:, 8:9]))
                        dve.wait_ge(S[f"x_in_l{h}"], 16 * (k + 1))
                        dve.wait_ge(S[f"x1_out{h}"], 16 + 16 * k)
                        dve.wait_ge(S[f"f_made{h}"], UP + k)
                        made[0] += 1
                        V.scalar_tensor_tensor(out=x1t[h][:], in0=acc[:, col, 0:D].rearrange("p a d -> p (a d)"),
                                               scalar=sm[:, 8:9], in1=xt[h][:],
                                               op0=ALU.mult, op1=ALU.add).then_inc(S["dve_c"], 1)
                        dve.wait_ge(S["dve_c"], made[1] + made[0])
                        dve.sem_inc(S[f"x1_made{h}"], 1)
                        made[0] += 1
                        V.bn_stats(stats[:, 0, :], x1t[h][:]).then_inc(S["dve_c"], 1)
                        dve.wait_ge(S["dve_c"], made[1] + made[0])
                        settle(dve)
                        own(V.bn_aggr(mv[:, 0, :], stats[:, 0, :]))
                        V.tensor_scalar(sm[:, 9:10], mv[:, 0, 1:2], 1e-5, None, ALU.add).then_inc(S["std1_in"], 1)
                        dve.wait_ge(S["std1_made"], i + 1)
                        V.reciprocal(rstd1[:, col], sm[:, 10:11]).then_inc(S["scaled1"], 1)
                        dve.wait_ge(S["scaled1"], 2 * i + 1)
                        V.scalar_tensor_tensor(out=nmr1[:, col], in0=mv[:, 0, 0:1], scalar=-1.0, in1=rstd1[:, col],
                                               op0=ALU.mult, op1=ALU.mult).then_inc(S["scaled1"], 1)
                        dve.wait_ge(S["hist_ps"], UP + i + 1)
                        V.scalar_tensor_tensor(out=outdeg[:], in0=ps_h[0:P, 0:NB], scalar=first[0:P, bass.ds(r, 1)],
                                               in1=outdeg[:], op0=ALU.mult, op1=ALU.add).then_inc(S["hist_made"], 1)
                        assert made[0] == n_own, made[0]
            steps0 = R * NB
            dve.wait_ge(S["hist_made"], UP + steps0)
            start0 = start + steps0 * n_own
            made[0], made[1] = 0, start0
            V.tensor_scalar(outdeg[:], outdeg[:], 1.0, None, ALU.max).then_inc(S["deg_made"], 1)
            own(V.tensor_scalar(filled[:].unsqueeze(2), acc[:, :, D:D + 1], 0.0, None, ALU.is_gt))
            dve.wait_ge(S["sod_made"], 1)
            V.reciprocal(rso[:], sod[:]).then_inc(S["rs_made"], 1)
            dve.wait_ge(S["rs_made"], 1)
            n_pre = made[0]
            n_own = 8
            with dve.Fori(0, R) as r:
                with dve.Fori(0, XH) as p:
                    j = r * XH + p
                    k = j + R * XH
                    for h in range(2):
                        i, b = 2 * j + h, 2 * p + h
                        col = bass.ds(b, 1)
                        made[0], made[1] = 0, start0 + n_pre + i * n_own
                        w = wts[h]
                        dve.wait_ge(S[f"edge_in{h}"], 16 * (k + 1))
                        made[0] += 1
                        V.tensor_scalar(ndl[h][:].unsqueeze(2), edge[h][:, :, 1:2].bitcast(f32), base[:, col], None,
                                        ALU.subtract).then_inc(S["dve_c"], 1)
                        dve.wait_ge(S["dve_c"], made[1] + made[0])
                        dve.sem_inc(S[f"ndl_made{h}"], 1)
                        dve.wait_ge(S[f"used{h}1"], UP + k)
                        own(V.tensor_tensor(w[:], over_tiles(slot[:, 0:P], T, P), over_slots(ndl[h][:], T, P), ALU.is_equal))
                        for c in range(2):
                            part_ = w[:, c * TC:(c + 1) * TC, :]
                            dve.wait_ge(S[f"got{h}{c}"], TC * 16 * (k + 1))
                            V.tensor_tensor(part_, part_,
                                            rows[h][:, c * TC:(c + 1) * TC, RS:RS + 1].to_broadcast([128, TC, P]),
                                            ALU.mult).then_inc(S[f"w_made{h}{c}"], 1)
                        dve.wait_ge(S[f"used{h}1"], UP + k + 1)
                        av = acc[:, col, 0:D].rearrange("p a d -> p (a d)")
                        own(V.scalar_tensor_tensor(out=av, in0=av, scalar=later[0:P, bass.ds(r, 1)],
                                                   in1=ps_a[h][0:P, 0:D], op0=ALU.mult, op1=ALU.add))
                        dve.wait_ge(S[f"f2_made{h}"], j + 1)
                        V.scalar_tensor_tensor(out=U[h][:], in0=av, scalar=rso[:, col], in1=F[h][:],
                                               op0=ALU.mult, op1=ALU.add).then_inc(S["up_made"], 1)
                        V.scalar_tensor_tensor(out=F[h][:], in0=av, scalar=rso[:, col], in1=F[h][:],
                                               op0=ALU.mult, op1=ALU.mult).then_inc(S["up_made"], 1)
                        dve.wait_ge(S["o_ps"], i + 1)
                        dve.wait_ge(S[f"y_out{h}"], 16 + 16 * j)
                        own(V.scalar_tensor_tensor(out=y[h][:], in0=ps_o[0:P, 0:D], scalar=filled[:, col], in1=b1_s[:],
                                                   op0=ALU.mult, op1=ALU.add))
                        dve.sem_inc(S["o_read"], 1)
                        own(V.scalar_tensor_tensor(out=y[h][:], in0=y[h][:], scalar=0.01, in1=y[h][:],
                                                   op0=ALU.mult, op1=ALU.max))
                        V.tensor_tensor_reduce(out=junk[:], in0=y[h][:], in1=y[h][:], scale=1.0, scalar=0.0,
                                               op0=ALU.mult, op1=ALU.add, accum_out=sm[:, 0:1]).then_inc(S["ss_made"], 1)
                        dve.wait_ge(S["norm_made"], i + 1)
                        own(V.tensor_scalar(sm[:, 1:2], sm[:, 2:3], 1e-12, None, ALU.max))
                        own(V.reciprocal(sm[:, 3:4], sm[:, 1:2]))
                        dve.wait_ge(S[f"x1_in{h}"], 16 * (j + 1))
                        own(V.scalar_tensor_tensor(out=y[h][:], in0=y[h][:], scalar=sm[:, 3:4], in1=xt[h][:],
                                                   op0=ALU.mult, op1=ALU.add))
                        dve.sem_inc(S[f"y_made{h}"], 1)
                        assert made[0] == n_own, made[0]

        @block.scalar
        def _(act):
            A = nc.scalar
            for w_s, w_d in ((Wv_s, Wv), (W1_s, W1), (W2_s, W2)):
                act.dma_start(w_s[:], w_d.rearrange("(c p) n -> p c n", p=128)).then_inc(S["consts_in"], 16)
            for r_s, r_d in ((bv_s, bv), (wq_s, wq), (wk_s, wk), (b1_s, b1)):
                act.dma_start(r_s[:], r_d.unsqueeze(0).to_broadcast([P, D])).then_inc(S["consts_in"], 16)
            for c, s_d in enumerate((bq, bk)):
                act.dma_start(bqk[:, c:c + 1], s_d.unsqueeze(0).to_broadcast([P, 1])).then_inc(S["consts_in"], 16)
            for n, name in enumerate(stores):
                act.dma_start(primed[:, n:n + 1], bq.unsqueeze(0)).then_inc(S[name], 16)
            act.wait_ge(S["pre_std"], 1)
            A.activation(rstd[:], nmr[:], ACT.Sqrt).then_inc(S["pre_rstd"], 1)
            act.wait_ge(S["pre_scaled"], 1)
            for t in range(NB):
                h = t % 2
                if t >= 2:
                    act.wait_ge(S["hn_T"], t - 1)
                A.activation(hn[h][:], xs[t // XH][:, t % XH, :], ACT.Relu, bias=nmr[:, t:t + 1],
                             scale=rstd[:, t:t + 1]).then_inc(S["hn_made"], 1)
                act.wait_ge(S["hn_T"], t + 1)
                A.activation(hT[h][:, 0:2, :], ps_tt[h][:, 0:2, 0:P], ACT.Copy).then_inc(S["hT_made"], 1)
            act.wait_ge(S["windows_out"], 16)
            R = rounds(act)
            with act.Fori(0, R) as r:
                with act.Fori(0, XH) as p:
                    k = r * XH + p
                    for h in range(2):
                        i, b = 2 * k + h, 2 * p + h
                        col = bass.ds(b, 1)
                        act.wait_ge(S[f"ndl_made{h}"], UP + k + 1)
                        act.wait_ge(S[f"used{h}1"], UP + k)
                        for t in range(T):
                            last = A.activation(wts[h][:, t, :], slot[:, 0:P], ACT.Square, bias=ndl[h][:, t:t + 1])
                        last.then_inc(S[f"sq_made{h}"], 1)
                        act.wait_ge(S["corr_in"], i + 1)
                        A.activation(sm[:, 7:8], sm[:, 6:7], ACT.Exp).then_inc(S["corr_made"], 1)
                        for c in range(2):
                            act.wait_ge(S[f"e_made{c}"], UP + i + 1)
                            part_ = wts[h][:, c * TC:(c + 1) * TC, :]
                            A.activation(part_, part_, ACT.Exp).then_inc(S[f"w_made{h}{c}"], 1)
                        act.wait_ge(S["std1_in"], i + 1)
                        A.activation(sm[:, 10:11], sm[:, 9:10], ACT.Sqrt).then_inc(S["std1_made"], 1)
                        act.wait_ge(S["scaled1"], 2 * i + 2)
                        act.wait_ge(S[f"f_out{h}"], 16 + 16 * k)
                        A.activation(trow[h][:, 0:D], x1t[h][:], ACT.Relu, bias=nmr1[:, col],
                                     scale=rstd1[:, col]).then_inc(S[f"f_made{h}"], 1)
                        rows_of = bass.ds(b * P, P)
                        act.dma_start(x1d[rows_of, :], x1t[h][:]).then_inc(S[f"x1_out{h}"], 16)
                        act.wait_ge(S[f"f_made{h}"], UP + k + 1)
                        act.dma_start(tab1[rows_of, :], trow[h][:]).then_inc(S[f"f_out{h}"], 16)
            act.wait_ge(S["deg_made"], 1)
            A.activation(sod[:], outdeg[:], ACT.Sqrt).then_inc(S["sod_made"], 1)
            with act.Fori(0, R) as r:
                with act.Fori(0, XH) as p:
                    j = r * XH + p
                    for h in range(2):
                        i, b = 2 * j + h, 2 * p + h
                        col = bass.ds(b, 1)
                        act.wait_ge(S[f"x1_in{h}"], 16 * (j + 1))
                        act.wait_ge(S["upT_made"], UP + i)
                        A.activation(F[h][:], xt[h][:], ACT.Relu, bias=nmr1[:, col],
                                     scale=rstd1[:, col]).then_inc(S[f"f2_made{h}"], 1)
                        act.wait_ge(S["upT_made"], UP + i + 1)
                        A.activation(hT[h][:], ps_t[:, :, 0:P], ACT.Copy).then_inc(S["upT_copied"], 1)
                        act.wait_ge(S["ss_made"], i + 1)
                        A.activation(sm[:, 2:3], sm[:, 0:1], ACT.Sqrt).then_inc(S["norm_made"], 1)
                        act.wait_ge(S[f"y_made{h}"], UP + j + 1)
                        act.dma_start(out[bass.ds(b * P, P), :], y[h][:]).then_inc(S[f"y_out{h}"], 16)

        @block.tensor
        def _(pe):
            TE = nc.tensor
            for name in counters:
                pe.sem_inc(S[name], UP)
            pe.wait_ge(S["dve_iota"], 1)
            pe.wait_ge(S["consts_in"], 9 * 16)
            with pe.Fori(0, XH) as p:
                for h in range(2):
                    t = 2 * p + h
                    pe.wait_ge(S["hn_made"], t + 1)
                    if h == 0:
                        pe.wait_ge(S["hT_made"], UP + 2 * p)
                    for c in range(2):
                        last = TE.transpose(ps_tt[h][:, c, 0:P], hn[h][:, c * 128:(c + 1) * 128], ident[0:P, 0:P])
                    last.then_inc(S["hn_T"], 1)
                    pe.wait_ge(S["hT_made"], UP + t + 1)
                    if h == 0:
                        pe.wait_ge(S["h_row"], UP + 2 * p)
                    for c in range(2):
                        last = TE.matmul(ps_a[h][0:P, 0:D], hT[h][:, c, :], Wv_s[:, c, :], start=(c == 0), stop=(c == 1))
                    last.then_inc(S["h_ps"], 1)
            pe.wait_ge(S["windows_made"], 1)
            pe.wait_ge(S["h_row"], UP + NB)
            R = rounds(pe)

            def sums(h, k, width):
                for c in range(2):
                    pe.wait_ge(S[f"w_made{h}{c}"], UP + k + 1)
                    for t in range(c * TC, (c + 1) * TC):
                        last = TE.matmul(ps_a[h][0:P, 0:width], wts[h][:, t, :], rows[h][:, t, 0:width],
                                         start=(t == 0), stop=(t == T - 1))
                    last.then_inc(S[f"used{h}{c}"], 1)

            with pe.Fori(0, R) as r:
                with pe.Fori(0, XH) as p:
                    k = r * XH + p
                    for h in range(2):
                        i = 2 * k + h
                        pe.wait_ge(S["dk_made"], i + 1)
                        pe.wait_ge(S["e_made1"], UP + i)
                        TE.matmul(ps_k[:, 0:P], ones[0:P, :], dk[:], start=True, stop=True).then_inc(S["kb_made"], 1)
                        pe.wait_ge(S["half_max"], i + 1)
                        TE.transpose(ps_q[0:P, 0:128], qm[:, 2, :], ident[:]).then_inc(S["qT_made"], 1)
                        pe.wait_ge(S["dm_made"], i + 1)
                        TE.matmul(ps_m[:, 0:P], ones[0:P, :], dm[:], start=True, stop=True).then_inc(S["mb_made"], 1)
                        sums(h, k, D + 1)
                        pe.wait_ge(S["oh_made"], 2 * i + 2)
                        pe.wait_ge(S["hist_made"], UP + i)
                        for t in range(HT):
                            last = TE.matmul(ps_h[0:P, 0:NB], oh_lo[:, t, :], oh_hi[:, t, :], start=(t == 0), stop=(t == HT - 1))
                        last.then_inc(S["hist_ps"], 1)
            with pe.Fori(0, R) as r:
                with pe.Fori(0, XH) as p:
                    j = r * XH + p
                    k = j + R * XH
                    for h in range(2):
                        i = 2 * j + h
                        sums(h, k, D)
                        pe.wait_ge(S["up_made"], 2 * i + 2)
                        pe.wait_ge(S["upT_copied"], UP + i)
                        for c in range(4):
                            m = (U, F)[c // 2][h]
                            last = TE.transpose(ps_t[:, c, 0:P], m[:, c % 2 * 128:(c % 2 + 1) * 128], ident[0:P, 0:P])
                        last.then_inc(S["upT_made"], 1)
                        pe.wait_ge(S["upT_copied"], UP + i + 1)
                        pe.wait_ge(S["o_read"], UP + i)
                        for c in range(4):
                            last = TE.matmul(ps_o[0:P, 0:D], hT[h][:, c, :], (W1_s, W2_s)[c // 2][:, c % 2, :],
                                             start=(c == 0), stop=(c == 3))
                        last.then_inc(S["o_ps"], 1)


_INS = ["x", "src", "dst", "L0_gnn_Wv", "L0_gnn_bv", "L0_gnn_wq", "L0_gnn_bq", "L0_gnn_wk", "L0_gnn_bk",
        "L1_gnn_W1", "L1_gnn_W2", "L1_gnn_b"]


def kernel(**inputs):
    import numpy as _np
    import concourse.bacc as _bacc
    from concourse import mybir as _mybir
    from concourse.bass_utils import run_bass_kernel_spmd as _run

    nc = _bacc.Bacc("TRN2", target_bir_lowering=False, num_devices=1)
    arrays, args = {}, []
    for name in _INS:
        a = _np.ascontiguousarray(inputs[name])
        if a.ndim == 0:
            a = a.reshape(1)
        arrays[f"in_{name}"] = a
        args.append(nc.dram_tensor(f"in_{name}", a.shape, _mybir.dt.from_np(a.dtype), kind="ExternalInput").ap())
    args.append(nc.dram_tensor("out_0", (N, D), _mybir.dt.float32, kind="ExternalOutput").ap())
    gnn(nc, *args)
    r = _run(nc, [arrays], core_ids=[0])
    return r.results[0]["out_0"]
```

```python
import concourse.bass as bass
from concourse import mybir
from contextlib import ExitStack

N, D, E = 6250, 256, 200000
P = 125
NB = N // P
T = 34
TC = T // 2
WIN = T * 128
RMAX = -(-E // WIN)
TW = 264
ONE, QC, RS = D, D + 1, D
EC = E // P
SPL = 160
NS = E // SPL
HT = EC // NB
BIG = 1e28
NODST = 7000.0
UP = 1
MAGIC = 12582912.0


def gnn(nc, x, src, dst, Wv, bv, wq, bq, wk, bk, W1, W2, b1, out):
    f32, bf16, i32, u32, u8 = mybir.dt.float32, mybir.dt.bfloat16, mybir.dt.int32, mybir.dt.uint32, mybir.dt.uint8
    i16 = mybir.dt.int16
    ALU, ACT, AX = mybir.AluOpType, mybir.ActivationFunctionType, mybir.AxisListType

    edges = nc.dram_tensor("edges", (E + WIN, 2), i32).ap()
    dst16 = nc.dram_tensor("dst16", (E + WIN,), i16).ap()
    accd = nc.dram_tensor("accd", (N, D + 1), f32).ap()
    splits = nc.dram_tensor("splits", (NS,), f32).ap()
    startd = nc.dram_tensor("startd", (NB + 1,), f32).ap()
    wind = nc.dram_tensor("wind", (1, RMAX * NB), i32).ap()
    tab0 = nc.dram_tensor("tab0", (N, TW), f32).ap()
    tab1 = nc.dram_tensor("tab1", (N, TW), f32).ap()
    x1d = nc.dram_tensor("x1d", (N, D), f32).ap()

    ctx = ExitStack()
    with ctx:
        def sb(name, shape, dt=f32):
            return ctx.enter_context(nc.sbuf_tensor(name, shape, dt))

        def pb(name, shape, dt=f32):
            return ctx.enter_context(nc.psum_tensor(name, shape, dt))

        def sem(name):
            return ctx.enter_context(nc.semaphore(name))

        rows = [sb(f"rows{h}", [128, T, TW]) for h in range(2)]
        wts = [sb(f"wts{h}", [128, T, P]) for h in range(2)]
        acc_old = [sb(f"acc_old{h}", [P, D + 1]) for h in range(2)]
        acc_new = [sb(f"acc_new{h}", [P, D + 1]) for h in range(2)]
        dT = [sb(f"dT{h}", [P, WIN], i16) for h in range(2)]
        node_i = sb("node_i", [P, NB], i32)
        node = sb("node", [P, NB])
        k3 = sb("k3", [P, NB, 3], bf16)
        k_rest = sb("k_rest", [P, NB])
        m3 = sb("m3", [P, 3], bf16)
        ew = [sb(f"ew{h}", [128, 6, T]) for h in range(2)]
        d16 = sb("d16", [P, EC], i16)
        pad16 = sb("pad16", [128, T], i16)
        edge = [sb(f"edge{h}", [128, T, 2], i32) for h in range(2)]
        ndl = [sb(f"ndl{h}", [128, T]) for h in range(2)]
        oh_lo_m = sb("oh_lo_m", [P, HT * P], bf16)
        oh_lo = oh_lo_m[:].rearrange("p (t s) -> p t s", s=P)
        oh_hi = sb("oh_hi", [P, HT, NB], bf16)
        src_lo = sb("src_lo", [P, EC], u8)
        src_hi = sb("src_hi", [P, EC], u8)
        slot_i = sb("slot_i", [128, 128], i32)
        slot = sb("slot", [128, 128])
        slot_b = sb("slot_b", [128, 128], bf16)
        part_i = sb("part_i", [128, 1], i32)
        part = sb("part", [128, 1])
        ident = sb("ident", [128, 128])
        base_i = sb("base_i", [128, NB], i32)
        base = sb("base", [128, NB])
        thr = sb("thr", [128, 1])
        first = sb("first", [128, RMAX + 1])
        later = sb("later", [128, RMAX + 1])
        rstep_i = sb("rstep_i", [1, RMAX + 1], i32)
        rstep = sb("rstep", [1, RMAX + 1])
        Wv_s = sb("Wv_s", [128, 2, D])
        W1_s = sb("W1_s", [128, 2, D])
        W2_s = sb("W2_s", [128, 2, D])
        bv_s, wq_s, wk_s, b1_s = (sb(n, [P, D]) for n in ("bv_s", "wq_s", "wk_s", "b1_s"))
        primed = sb("primed", [1, 12])
        bqk = sb("bqk", [P, 2])
        mv = sb("mv", [P, NB, 2])
        rstd = sb("rstd", [P, NB])
        nmr = sb("nmr", [P, NB])
        rstd1 = sb("rstd1", [P, NB])
        nmr1 = sb("nmr1", [P, NB])
        kcol = sb("kcol", [P, NB])
        mcol = sb("mcol", [P, NB])
        outdeg = sb("outdeg", [P, NB])
        sod = sb("sod", [P, NB])
        rso = sb("rso", [P, NB])
        filled = sb("filled", [P, NB])
        stats = sb("stats", [P, NB, 6])
        hn = [sb(f"hn{h}", [P, D]) for h in range(2)]
        hT = [sb(f"hT{h}", [128, 4, P]) for h in range(2)]
        trow = [sb(f"trow{h}", [P, TW]) for h in range(2)]
        junk = sb("junk", [P, D])
        xt = [sb(f"xt{h}", [P, D]) for h in range(2)]
        x1t = [sb(f"x1t{h}", [P, D]) for h in range(2)]
        U, F = x1t, hn
        y = [sb(f"y{h}", [P, D]) for h in range(2)]
        qm = sb("qm", [128, 3, P])
        sc = sb("sc", [P, 8])
        corr = [sb(f"corr{h}", [P, 2]) for h in range(2)]
        sf = sb("sf", [P, 6])
        sm = sb("sm", [P, 4])
        spl_s = sb("spl_s", [P, EC // SPL])
        cnt = sb("cnt", [NB + 1, 6])
        chunk = sb("chunk", [NB + 1, SPL], i32)
        chunk_f = sb("chunk_f", [NB + 1, SPL])
        chunk_i = sb("chunk_i", [NB + 1, 1], u32)
        st_row = sb("st_row", [1, NB + 1])
        gap = sb("gap", [1, NB])
        rnd_f = sb("rnd_f", [1, RMAX + 4])
        rnd = sb("rnd", [1, 1], i32)
        padi = sb("padi", [128, T, 2], i32)

        win = wts[1][0:1, :, :].rearrange("p a b -> p (a b)")[:, 0:RMAX * NB].bitcast(i32)
        spl_b = oh_lo_m[0:NB + 1, 0:2 * NS].bitcast(f32)
        srcs = wts[0][0:P, :, :].rearrange("p a b -> p (a b)")[:, 0:EC].bitcast(i32)
        dsts = wts[0][0:P, :, :].rearrange("p a b -> p (a b)")[:, EC:2 * EC].bitcast(i32)
        pairs = wts[1][0:P, :, :].rearrange("p a b -> p (a b)")[:, 0:2 * EC].bitcast(i32) \
            .rearrange("p (e c) -> p e c", c=2)
        tmp_hi = rows[0][0:P, :, :].rearrange("p a b -> p (a b)")[:, T * TW - EC:T * TW]
        tmp_lo = rows[1][0:P, :, :].rearrange("p a b -> p (a b)")[:, T * TW - EC:T * TW]
        XH = NB // 2
        xs = [rows[h][0:P, :, :].rearrange("p a b -> p (a b)")[:, 0:XH * D]
              .rearrange("p (t d) -> p t d", d=D) for h in range(2)]

        ps_q = pb("ps_q", [128, 512])
        ps_k = pb("ps_k", [128, 512])
        ps_m = pb("ps_m", [128, 512])
        ps_h = pb("ps_h", [128, 512])
        ps_a = [pb(f"ps_a{h}", [128, 512]) for h in range(2)]
        ps_t = pb("ps_t", [128, 4, 128])
        ps_o = pb("ps_o", [128, 512])
        ps_tt = [ps_t[:], ps_o[:].rearrange("p (c n) -> p c n", n=128)]

        names = """edges_in consts_in x_in0 x_in1 xhalf iotas dve_iota pairs_made pairs_out pads_made split_made
            split_out split_in chunk_at chunk_in start_made start_out start_in windows_made windows_out lohi
            pre_std pre_rstd pre_scaled hn_made hn_T hT_made h_ps h_row pre_tab
            edge_in0 edge_in1 ndl_made0 ndl_made1 sq_made0 sq_made1 got00 got01 got10 got11
            used00 used01 used10 used11 half_max qT_made m3_made ke_made me_made ohT_made dst16_out zero_out dT_in0 dT_in1 acc_in0 acc_in1 acc_out0 acc_out1 acc_made0 acc_made1 lw_made w_read k3_made dve_f
            e_made0 e_made1 w_made00 w_made01 w_made10 w_made11 corr_in corr_made
            oh_made hist_ps hist_made x_in_l0 x_in_l1 x1_made0 x1_made1 std1_in std1_made
            scaled1 f_made0 f_made1 f_out0 f_out1 x1_out0 x1_out1 deg_made sod_made rs_made rs_out
            eq_made x1_in0 x1_in1 f2_made0 f2_made1 up_made upT_made upT_copied o_ps o_read ss_made norm_made
            y_out0 y_out1 y_made0 y_made1 settled dve_c pool_c""".split()
        S = {n: sem(n) for n in names}
        counters = """used00 used01 used10 used11 ndl_made0 ndl_made1 x1_made0 x1_made1 f_made0 f_made1
            hist_ps hist_made y_made0 y_made1 upT_made upT_copied o_read hT_made h_row
            w_made00 w_made01 w_made10 w_made11 acc_made0 acc_made1 me_made""".split()
        stores = "x1_out0 x1_out1 f_out0 f_out1 y_out0 y_out1 pre_tab acc_out0 acc_out1".split()

        def flat(t):
            return t.rearrange("p a b -> p (a b)")

        def over_tiles(col, n, w):
            return col.unsqueeze(1).to_broadcast([col.shape[0], n, w])

        def over_slots(col, n, w):
            return col.unsqueeze(2).to_broadcast([col.shape[0], n, w])

        def settle(eng):
            eng.sem_inc(S["settled"], 1)

        def rounds(eng):
            return eng.value_load(rnd[0:1, 0:1], min_val=1, max_val=RMAX)

        block = ctx.enter_context(nc.Block())

        @block.sync
        def _(sp):
            sp.dma_start(dsts, dst.rearrange("(p e) -> p e", p=P)).then_inc(S["edges_in"], 16)
            sp.dma_start(srcs, src.rearrange("(p e) -> p e", p=P)).then_inc(S["edges_in"], 16)
            xv = x.rearrange("(t p) d -> p t d", p=P)
            for h in range(2):
                sp.dma_start(xs[h], xv[:, h * XH:(h + 1) * XH, :]).then_inc(S[f"x_in{h}"], 16)
            sp.wait_ge(S["split_made"], 1)
            sp.dma_start(splits.rearrange("(p s) -> p s", p=P), spl_s[:]).then_inc(S["split_out"], 16)
            sp.wait_ge(S["split_out"], 16)
            sp.dma_start(spl_b, splits.unsqueeze(0).to_broadcast([NB + 1, NS])).then_inc(S["split_in"], 16)
            sp.wait_ge(S["pairs_made"], 1)
            sp.dma_start(edges[0:E, :].rearrange("(p e) c -> p e c", p=P), pairs).then_inc(S["pairs_out"], 16)
            sp.wait_ge(S["pads_made"], 1)
            sp.dma_start(edges[E:E + WIN, :].rearrange("(p e) c -> p e c", p=128), padi[:]).then_inc(S["pairs_out"], 16)
            sp.wait_ge(S["split_made"], 2)
            sp.dma_start(dst16[0:E].rearrange("(p e) -> p e", p=P), d16[:]).then_inc(S["dst16_out"], 16)
            sp.dma_start(dst16[E:E + WIN].rearrange("(p e) -> p e", p=128), pad16[:]).then_inc(S["dst16_out"], 16)
            sp.dma_start(accd.rearrange("(t p) c -> p t c", p=P), over_tiles(acc_new[0][:], NB, D + 1)) \
                .then_inc(S["zero_out"], 16)
            sp.wait_ge(S["start_made"], 1)
            sp.dma_start(startd.unsqueeze(1), cnt[:, 4:5]).then_inc(S["start_out"], 16)
            sp.wait_ge(S["start_out"], 16)
            sp.dma_start(st_row[:], startd.unsqueeze(0)).then_inc(S["start_in"], 16)
            sp.wait_ge(S["pairs_out"], 32)
            sp.wait_ge(S["windows_made"], 1)
            sp.dma_start(wind, win).then_inc(S["windows_out"], 16)
            with sp.Fori(0, XH) as p:
                for h in range(2):
                    sp.wait_ge(S["h_row"], UP + 2 * p + h + 1)
                    sp.dma_start(tab0[bass.ds((2 * p + h) * P, P), :], trow[h][:]).then_inc(S["pre_tab"], 16)
            sp.wait_ge(S["windows_out"], 16)
            R = rounds(sp)
            sp.wait_ge(S["pre_tab"], 16 + 16 * NB)
            sp.wait_ge(S["dst16_out"], 32)
            sp.wait_ge(S["zero_out"], 16)

            def window(r, b, k, h):
                e0 = sp.value_load(wind[0:1, bass.ds(r * NB + b, 1)], min_val=0, max_val=E)
                sp.wait_ge(S[f"w_made{h}1"], UP + k)
                sp.dma_start(edge[h][:], edges[bass.ds(e0, WIN), :].rearrange("(p e) c -> p e c", p=128)) \
                    .then_inc(S[f"edge_in{h}"], 16)
                return e0

            def sums_so_far(b, k, h):
                sp.wait_ge(S[f"acc_made{h}"], UP + k)
                settle(sp)
                sp.wait_ge(S[f"acc_out{h}"], 16 + 16 * k)
                sp.dma_start(acc_old[h][:], accd[bass.ds(b * P, P), :]).then_inc(S[f"acc_in{h}"], 16)

            with sp.Fori(0, R) as r:
                with sp.Fori(0, XH) as p:
                    k = r * XH + p
                    for h in range(2):
                        e0 = window(r, 2 * p + h, k, h)
                        sp.dma_start(dT[h][:], dst16[bass.ds(e0, WIN)].unsqueeze(0).to_broadcast([P, WIN])) \
                            .then_inc(S[f"dT_in{h}"], 16)
                        sp.wait_ge(S[f"x1_made{h}"], UP + k)
                        sp.dma_start(xt[h][:], x[bass.ds((2 * p + h) * P, P), :]).then_inc(S[f"x_in_l{h}"], 16)
                        sums_so_far(2 * p + h, k, h)
            KR = R * XH
            for h in range(2):
                sp.wait_ge(S[f"x1_out{h}"], 16 + KR * 16)
            sp.wait_ge(S["f_out0"], 16 + KR * 16)
            sp.wait_ge(S["f_out1"], 16 + KR * 16)
            sp.wait_ge(S["rs_made"], 1)
            with nc.allow_non_contiguous_dma(reason="one column of the table"):
                sp.dma_start(tab1.rearrange("(t p) c -> p t c", p=P)[:, :, RS:RS + 1], rso[:].unsqueeze(2)) \
                    .then_inc(S["rs_out"], 16)
            with sp.Fori(0, R) as r:
                with sp.Fori(0, XH) as p:
                    k = r * XH + p + KR
                    for h in range(2):
                        window(r, 2 * p + h, k, h)
                        sp.wait_ge(S[f"y_made{h}"], UP + r * XH + p)
                        sp.dma_start(xt[h][:], x1d[bass.ds((2 * p + h) * P, P), :]).then_inc(S[f"x1_in{h}"], 16)
                        sums_so_far(2 * p + h, k, h)
            for h in range(2):
                sp.wait_ge(S[f"y_out{h}"], 16 + KR * 16)
                sp.wait_ge(S[f"acc_out{h}"], 16 + 2 * KR * 16)
            settle(sp)

        @block.gpsimd
        def _(pool):
            nc.gpsimd.iota(slot_i[:], [[1, 128]], base=0, channel_multiplier=0).then_inc(S["iotas"], 1)
            nc.gpsimd.iota(part_i[:], [[0, 1]], base=0, channel_multiplier=1).then_inc(S["iotas"], 1)
            nc.gpsimd.iota(base_i[:], [[P, NB]], base=0, channel_multiplier=0).then_inc(S["iotas"], 1)
            nc.gpsimd.iota(rstep_i[:], [[WIN, RMAX + 1]], base=0, channel_multiplier=0).then_inc(S["iotas"], 1)
            nc.gpsimd.memset(acc_new[0][:], 0.0).then_inc(S["iotas"], 1)
            nc.gpsimd.iota(node_i[:], [[P, NB]], base=0, channel_multiplier=1).then_inc(S["iotas"], 1)
            nc.gpsimd.memset(later[:, 0:1], 0.0).then_inc(S["iotas"], 1)
            nc.gpsimd.memset(later[:, 1:RMAX + 1], 1.0).then_inc(S["iotas"], 1)
            nc.gpsimd.memset(first[:, 0:1], 1.0).then_inc(S["iotas"], 1)
            nc.gpsimd.memset(first[:, 1:RMAX + 1], 0.0).then_inc(S["iotas"], 1)
            nc.gpsimd.memset(outdeg[:], 0.0).then_inc(S["iotas"], 1)
            nc.gpsimd.memset(mcol[:], -1e30).then_inc(S["iotas"], 1)
            for h in range(2):
                nc.gpsimd.memset(trow[h][:, D:TW], 0.0).then_inc(S["pool_c"], 1)
                pool.wait_ge(S["pool_c"], h + 1)
                nc.gpsimd.memset(trow[h][:, ONE:ONE + 1], 1.0).then_inc(S["iotas"], 1)
            nc.gpsimd.memset(padi[:, :, 0:1], 0).then_inc(S["pool_c"], 1)
            nc.gpsimd.memset(padi[:, :, 1:2].bitcast(f32), NODST).then_inc(S["pool_c"], 1)
            pool.wait_ge(S["pool_c"], 4)
            pool.sem_inc(S["pads_made"], 1)
            nc.gpsimd.memset(pad16[:], NODST).then_inc(S["iotas"], 1)
            pool.wait_ge(S["edges_in"], 32)
            nc.gpsimd.tensor_scalar(tmp_hi, srcs, 0.5, 1.0 / P, ALU.add, ALU.mult).then_inc(S["pool_c"], 1)
            pool.wait_ge(S["pool_c"], 5)
            nc.gpsimd.tensor_scalar(tmp_hi, tmp_hi, -0.5, None, ALU.add).then_inc(S["pool_c"], 1)
            pool.wait_ge(S["pool_c"], 6)
            nc.gpsimd.tensor_scalar(tmp_hi, tmp_hi, MAGIC, None, ALU.add).then_inc(S["pool_c"], 1)
            pool.wait_ge(S["pool_c"], 7)
            nc.gpsimd.tensor_scalar(tmp_hi, tmp_hi, -MAGIC, None, ALU.add).then_inc(S["pool_c"], 1)
            pool.wait_ge(S["pool_c"], 8)
            nc.gpsimd.tensor_copy(src_hi[:], tmp_hi).then_inc(S["lohi"], 1)
            nc.gpsimd.tensor_scalar(tmp_lo, tmp_hi, -float(P), None, ALU.mult).then_inc(S["lohi"], 1)
            pool.wait_ge(S["chunk_at"], 1)
            nc.gpsimd.indirect_dma_start(chunk[:], None, dst.rearrange("(a b) -> a b", b=1),
                                         bass.IndirectOffsetOnAxis(chunk_i[:], 0)).then_inc(S["chunk_in"], 16)
            pool.wait_ge(S["lohi"], 3)
            pool.wait_ge(S["pre_tab"], 16 + 16 * NB)
            pool.wait_ge(S["windows_made"], 1)
            R = rounds(pool)
            for layer in range(2):
                table = (tab0, tab1)[layer]
                if layer:
                    pool.wait_ge(S["rs_out"], 16)
                with pool.Fori(0, R) as r:
                    with pool.Fori(0, XH) as p:
                        k = r * XH + p + (R * XH if layer else 0)
                        for h in range(2):
                            pool.wait_ge(S[f"edge_in{h}"], 16 * (k + 1))
                            for c in range(2):
                                pool.wait_ge(S[f"used{h}{c}"], UP + k)
                                settle(pool)
                                for t in range(c * TC, (c + 1) * TC):
                                    nc.gpsimd.indirect_dma_start(
                                        rows[h][:, t, :], None, table,
                                        bass.IndirectOffsetOnAxis(edge[h][:, t, 0:1].bitcast(u32), 0)) \
                                        .then_inc(S[f"got{h}{c}"], 16)

        @block.vector
        def _(dve):
            V = nc.vector
            made = [0, 0]

            def own(ins):
                made[0] += 1
                ins.then_inc(S["dve_c"], 1)
                dve.wait_ge(S["dve_c"], made[1] + made[0])

            dve.wait_ge(S["edges_in"], 32)
            own(V.tensor_copy(pairs[:, :, 1:2].bitcast(f32), dsts.unsqueeze(2)))
            V.tensor_copy(spl_s[:], pairs[:, 0:EC:SPL, 1:2].bitcast(f32).rearrange("p e c -> p (e c)")).then_inc(S["split_made"], 1)
            V.tensor_copy(pairs[:, :, 0:1], srcs.unsqueeze(2)).then_inc(S["pairs_made"], 1)
            dve.wait_ge(S["iotas"], 15)
            V.tensor_copy(d16[:], dsts).then_inc(S["split_made"], 1)
            own(V.tensor_copy(node[:], node_i[:]))
            own(V.tensor_copy(slot[:], slot_i[:]))
            own(V.tensor_copy(slot_b[:], slot_i[:]))
            own(V.tensor_copy(part[:], part_i[:]))
            own(V.tensor_copy(base[:], base_i[:]))
            own(V.tensor_copy(rstep[:], rstep_i[:]))
            V.tensor_scalar(ident[:], slot[:], part[:, 0:1], None, ALU.is_equal).then_inc(S["dve_iota"], 1)
            own(V.tensor_scalar(thr[:], part[:], float(P), None, ALU.mult))
            dve.wait_ge(S["split_in"], 16)
            own(V.tensor_scalar(spl_b, spl_b, thr[0:NB + 1, 0:1], None, ALU.is_lt))
            own(V.tensor_reduce(cnt[:, 0:1], spl_b, AX.X, ALU.add))
            own(V.tensor_scalar(cnt[:, 1:2], cnt[:, 0:1], -1.0, 0.0, ALU.add, ALU.max))
            own(V.tensor_scalar(cnt[:, 2:3], cnt[:, 1:2], float(SPL), None, ALU.mult))
            V.tensor_copy(chunk_i[:], cnt[:, 2:3]).then_inc(S["chunk_at"], 1)
            for h in range(2):
                dve.wait_ge(S[f"x_in{h}"], 16)
                for t in range(XH):
                    last = V.bn_stats(stats[:, h * XH + t, :], xs[h][:, t, :])
                own(last)
            for t in range(NB):
                last = V.bn_aggr(mv[:, t, :], stats[:, t, :])
            own(last)
            own(V.tensor_scalar(nmr[:].unsqueeze(2), mv[:, :, 1:2], 1e-5, None, ALU.add))
            V.tensor_scalar(nmr[:], nmr[:], 1.0, None, ALU.mult).then_inc(S["pre_std"], 1)
            dve.wait_ge(S["pre_rstd"], 1)
            own(V.reciprocal(rstd[:], rstd[:]))
            own(V.tensor_tensor(nmr[:].unsqueeze(2), mv[:, :, 0:1], rstd[:].unsqueeze(2), ALU.mult))
            V.tensor_scalar(nmr[:], nmr[:], -1.0, None, ALU.mult).then_inc(S["pre_scaled"], 1)
            dve.wait_ge(S["chunk_in"], 16)
            own(V.tensor_copy(chunk_f[:], chunk[:]))
            own(V.tensor_scalar(chunk_f[:], chunk_f[:], thr[0:NB + 1, 0:1], None, ALU.is_lt))
            own(V.tensor_reduce(cnt[:, 3:4], chunk_f[:], AX.X, ALU.add))
            V.tensor_tensor(cnt[:, 4:5], cnt[:, 3:4], cnt[:, 2:3], ALU.add).then_inc(S["start_made"], 1)
            dve.wait_ge(S["lohi"], 2)
            V.tensor_tensor(src_lo[:], tmp_lo, srcs, ALU.add).then_inc(S["lohi"], 1)
            dve.wait_ge(S["start_in"], 16)
            dve.wait_ge(S["pairs_out"], 32)
            own(V.tensor_tensor(win.rearrange("p (r b) -> p r b", b=NB), over_tiles(st_row[:, 0:NB], RMAX, NB),
                                over_slots(rstep[:, 0:RMAX], RMAX, NB), ALU.add))
            own(V.tensor_scalar(win, win, float(E), None, ALU.min))
            own(V.tensor_tensor(gap[:], st_row[:, 1:NB + 1], st_row[:, 0:NB], ALU.subtract))
            own(V.tensor_reduce(rnd_f[:, 0:1], gap[:], AX.X, ALU.max))
            own(V.tensor_scalar(rnd_f[:, 2:2 + RMAX], rstep[:, 0:RMAX], rnd_f[:, 0:1], None, ALU.is_lt))
            own(V.tensor_reduce(rnd_f[:, 1:2], rnd_f[:, 2:2 + RMAX], AX.X, ALU.add))
            V.tensor_scalar(rnd[:], rnd_f[:, 1:2], 1.0, None, ALU.max).then_inc(S["windows_made"], 1)
            dve.wait_ge(S["consts_in"], 9 * 16)
            made[1], start = made[0], made[0]
            made[0] = 0
            n_own = 4
            with dve.Fori(0, XH) as p:
                for h in range(2):
                    made[0] = 0
                    made[1] = start + (2 * p + h) * n_own
                    t = 2 * p + h
                    dve.wait_ge(S["h_ps"], t + 1)
                    if h == 0:
                        dve.wait_ge(S["pre_tab"], 16 + 32 * p)
                    own(V.tensor_tensor(trow[h][:, 0:D], ps_a[h][0:P, 0:D], bv_s[:], ALU.add))
                    own(V.tensor_tensor_reduce(out=junk[:], in0=trow[h][:, 0:D], in1=wq_s[:], scale=1.0, scalar=0.0,
                                               op0=ALU.mult, op1=ALU.add, accum_out=sm[:, 0:1]))
                    own(V.tensor_tensor_reduce(out=junk[:], in0=trow[h][:, 0:D], in1=wk_s[:], scale=1.0, scalar=0.0,
                                               op0=ALU.mult, op1=ALU.add, accum_out=sm[:, 1:2]))
                    V.tensor_scalar(trow[h][:, QC:QC + 1], sm[:, 0:1], bqk[:, 0:1], None, ALU.add).then_inc(S["h_row"], 1)
                    own(V.tensor_scalar(kcol[:, bass.ds(t, 1)], sm[:, 1:2], bqk[:, 1:2], None, ALU.add))
                    assert made[0] == n_own
            dve.wait_ge(S["lohi"], 3)
            made[0], made[1] = 0, start + NB * n_own
            dve.wait_ge(S["h_row"], UP + NB)
            own(V.tensor_copy(k3[:, :, 0], kcol[:]))
            own(V.tensor_tensor(k_rest[:], kcol[:], k3[:, :, 0], ALU.subtract))
            own(V.tensor_copy(k3[:, :, 1], k_rest[:]))
            own(V.tensor_tensor(k_rest[:], k_rest[:], k3[:, :, 1], ALU.subtract))
            V.tensor_copy(k3[:, :, 2], k_rest[:]).then_inc(S["k3_made"], 1)
            R = rounds(dve)
            start += NB * n_own + 4
            n_own, n_fin = 17, 7
            finished = [0, 0]

            def own_f(ins):
                finished[0] += 1
                ins.then_inc(S["dve_f"], 1)
                dve.wait_ge(S["dve_f"], finished[1] + finished[0])

            def weigh(b, k, h):
                i, col = 2 * k + h, bass.ds(b, 1)
                made[0], made[1] = 0, start + i * n_own
                w, e = wts[h], ew[h]
                q = rows[h][:, :, QC:QC + 1].rearrange("p t c -> p (t c)")
                dve.wait_ge(S[f"edge_in{h}"], 16 * (k + 1))
                V.tensor_scalar(ndl[h][:].unsqueeze(2), edge[h][:, :, 1:2].bitcast(f32), -1.0, base[:, col],
                                ALU.mult, ALU.add).then_inc(S[f"ndl_made{h}"], 1)
                dve.wait_ge(S[f"dT_in{h}"], 16 * (k + 1))
                V.tensor_scalar(dT[h][:].bitcast(bf16), dT[h][:], node[:, col], None, ALU.is_equal) \
                    .then_inc(S["ohT_made"], 1)
                for c in range(2):
                    part_ = w[:, c * TC:(c + 1) * TC, :]
                    if c == 0:
                        dve.wait_ge(S[f"sq_made{h}"], k + 1)
                    dve.wait_ge(S[f"got{h}{c}"], TC * 16 * (k + 1))
                    own(V.scalar_tensor_tensor(
                        out=part_, in0=part_, scalar=-BIG,
                        in1=rows[h][:, c * TC:(c + 1) * TC, QC:QC + 1].to_broadcast([128, TC, P]),
                        op0=ALU.mult, op1=ALU.add))
                    own(V.tensor_reduce(qm[:, c, :], part_.rearrange("p t s -> p s t"), AX.X, ALU.max))
                V.tensor_tensor(qm[:, 2, :], qm[:, 0, :], qm[:, 1, :], ALU.max).then_inc(S["half_max"], 1)
                dve.wait_ge(S["ke_made"], i + 1)
                own(V.tensor_reduce(e[:, 0, :], ps_k[:, 0:3 * T].rearrange("p (t c) -> p t c", c=3), AX.X, ALU.add))
                own(V.tensor_tensor(e[:, 1, :], e[:, 0, :], q, ALU.add))
                own(V.scalar_tensor_tensor(out=e[:, 2, :], in0=e[:, 1, :], scalar=0.2, in1=e[:, 1, :],
                                           op0=ALU.mult, op1=ALU.max))
                own(V.tensor_tensor(e[:, 3, :], e[:, 2, :], q, ALU.subtract))
                dve.wait_ge(S["qT_made"], i + 1)
                own(V.tensor_reduce(sc[:, 0:1], ps_q[0:P, 0:128], AX.X, ALU.max))
                own(V.tensor_tensor(sc[:, 1:2], sc[:, 0:1], kcol[:, col], ALU.add))
                own(V.scalar_tensor_tensor(out=sc[:, 2:3], in0=sc[:, 1:2], scalar=0.2, in1=sc[:, 1:2],
                                           op0=ALU.mult, op1=ALU.max))
                own(V.tensor_tensor(sc[:, 3:4], sc[:, 2:3], mcol[:, col], ALU.max))
                own(V.tensor_copy(m3[:, 0:1], sc[:, 3:4]))
                own(V.tensor_tensor(sc[:, 4:5], sc[:, 3:4], m3[:, 0:1], ALU.subtract))
                own(V.tensor_copy(m3[:, 1:2], sc[:, 4:5]))
                own(V.tensor_tensor(sc[:, 5:6], sc[:, 4:5], m3[:, 1:2], ALU.subtract))
                V.tensor_copy(m3[:, 2:3], sc[:, 5:6]).then_inc(S["m3_made"], 1)
                V.tensor_tensor(corr[h][:, 0:1], mcol[:, col], sc[:, 3:4], ALU.subtract).then_inc(S["corr_in"], 1)
                dve.wait_ge(S["corr_in"], i + 1)
                own(V.tensor_tensor(mcol[:, col], sc[:, 3:4], sc[:, 3:4], ALU.max))
                dve.wait_ge(S["me_made"], UP + i + 1)
                V.tensor_reduce(e[:, 4, :], ps_m[:, 0:3 * T].rearrange("p (t c) -> p t c", c=3), AX.X, ALU.add) \
                    .then_inc(S["w_read"], 1)
                dve.wait_ge(S["w_read"], i + 1)
                V.tensor_tensor(e[:, 5, :], e[:, 3, :], e[:, 4, :], ALU.subtract).then_inc(S["lw_made"], 1)
                dve.wait_ge(S["hist_ps"], UP + i)
                cols = bass.ds(b * HT, HT)
                V.tensor_tensor(oh_lo, over_tiles(slot_b[0:P, 0:P], HT, P),
                                over_slots(src_lo[:, cols], HT, P), ALU.is_equal).then_inc(S["oh_made"], 1)
                V.tensor_tensor(oh_hi[:], over_tiles(slot_b[0:P, 0:NB], HT, NB),
                                over_slots(src_hi[:, cols], HT, NB), ALU.is_equal).then_inc(S["oh_made"], 1)
                assert made[0] == n_own, made[0]

            def finish(r, b, k, h):
                i, col = 2 * k + h, bass.ds(b, 1)
                finished[0], finished[1] = 0, i * n_fin
                dve.wait_ge(S["corr_made"], i + 1)
                dve.wait_ge(S[f"used{h}1"], UP + k + 1)
                dve.wait_ge(S[f"acc_in{h}"], 16 * (k + 1))
                dve.wait_ge(S[f"acc_out{h}"], 16 + 16 * k)
                V.scalar_tensor_tensor(out=acc_new[h][:], in0=acc_old[h][:], scalar=corr[h][:, 1:2],
                                       in1=ps_a[h][0:P, 0:D + 1], op0=ALU.mult, op1=ALU.add) \
                    .then_inc(S[f"acc_made{h}"], 1)
                dve.wait_ge(S[f"acc_made{h}"], UP + k + 1)
                own_f(V.tensor_scalar(sf[:, 0:1], acc_new[h][:, D:D + 1], 1e-30, None, ALU.max))
                own_f(V.tensor_scalar(filled[:, col], acc_new[h][:, D:D + 1], 0.0, None, ALU.is_gt))
                own_f(V.reciprocal(sf[:, 1:2], sf[:, 0:1]))
                dve.wait_ge(S[f"x_in_l{h}"], 16 * (k + 1))
                dve.wait_ge(S[f"x1_out{h}"], 16 + 16 * k)
                dve.wait_ge(S[f"f_made{h}"], UP + k)
                own_f(V.scalar_tensor_tensor(out=x1t[h][:], in0=acc_new[h][:, 0:D], scalar=sf[:, 1:2],
                                             in1=xt[h][:], op0=ALU.mult, op1=ALU.add))
                dve.sem_inc(S[f"x1_made{h}"], 1)
                own_f(V.bn_stats(stats[:, 0, :], x1t[h][:]))
                settle(dve)
                own_f(V.bn_aggr(mv[:, 0, :], stats[:, 0, :]))
                V.tensor_scalar(sf[:, 2:3], mv[:, 0, 1:2], 1e-5, None, ALU.add).then_inc(S["std1_in"], 1)
                dve.wait_ge(S["hist_ps"], UP + i + 1)
                V.scalar_tensor_tensor(out=outdeg[:], in0=ps_h[0:P, 0:NB], scalar=first[0:P, bass.ds(r, 1)],
                                       in1=outdeg[:], op0=ALU.mult, op1=ALU.add).then_inc(S["hist_made"], 1)
                dve.wait_ge(S["hist_made"], UP + i + 1)
                dve.wait_ge(S["std1_made"], i + 1)
                own_f(V.reciprocal(rstd1[:, col], sf[:, 3:4]))
                V.scalar_tensor_tensor(out=nmr1[:, col], in0=mv[:, 0, 0:1], scalar=-1.0, in1=rstd1[:, col],
                                       op0=ALU.mult, op1=ALU.mult).then_inc(S["scaled1"], 1)
                dve.wait_ge(S["scaled1"], i + 1)
                assert finished[0] == n_fin, finished[0]

            with dve.Fori(0, R) as r:
                weigh(0, r * XH, 0)
                with dve.Fori(0, XH - 1) as p:
                    k = r * XH + p
                    weigh(2 * p + 1, k, 1)
                    finish(r, 2 * p, k, 0)
                    weigh(2 * p + 2, k + 1, 0)
                    finish(r, 2 * p + 1, k, 1)
                weigh(NB - 1, r * XH + XH - 1, 1)
                finish(r, NB - 2, r * XH + XH - 1, 0)
                finish(r, NB - 1, r * XH + XH - 1, 1)
            steps0 = R * NB
            dve.wait_ge(S["hist_made"], UP + steps0)
            start0 = start + steps0 * n_own
            made[0], made[1] = 0, start0
            V.tensor_scalar(outdeg[:], outdeg[:], 1.0, None, ALU.max).then_inc(S["deg_made"], 1)
            dve.wait_ge(S["sod_made"], 1)
            V.reciprocal(rso[:], sod[:]).then_inc(S["rs_made"], 1)
            dve.wait_ge(S["rs_made"], 1)
            n_pre = made[0]
            n_own = 7
            with dve.Fori(0, R) as r:
                with dve.Fori(0, XH) as p:
                    j = r * XH + p
                    k = j + R * XH
                    for h in range(2):
                        i, b = 2 * j + h, 2 * p + h
                        col = bass.ds(b, 1)
                        made[0], made[1] = 0, start0 + n_pre + i * n_own
                        w = wts[h]
                        dve.wait_ge(S[f"edge_in{h}"], 16 * (k + 1))
                        made[0] += 1
                        V.tensor_scalar(ndl[h][:].unsqueeze(2), edge[h][:, :, 1:2].bitcast(f32), base[:, col], None,
                                        ALU.subtract).then_inc(S["dve_c"], 1)
                        dve.wait_ge(S["dve_c"], made[1] + made[0])
                        dve.sem_inc(S[f"ndl_made{h}"], 1)
                        dve.wait_ge(S[f"used{h}1"], UP + k)
                        own(V.tensor_tensor(w[:], over_tiles(slot[:, 0:P], T, P), over_slots(ndl[h][:], T, P), ALU.is_equal))
                        for c in range(2):
                            part_ = w[:, c * TC:(c + 1) * TC, :]
                            dve.wait_ge(S[f"got{h}{c}"], TC * 16 * (k + 1))
                            V.tensor_tensor(part_, part_,
                                            rows[h][:, c * TC:(c + 1) * TC, RS:RS + 1].to_broadcast([128, TC, P]),
                                            ALU.mult).then_inc(S[f"w_made{h}{c}"], 1)
                        dve.wait_ge(S[f"used{h}1"], UP + k + 1)
                        av = acc_new[h][:, 0:D]
                        dve.wait_ge(S[f"acc_in{h}"], 16 * (k + 1))
                        dve.wait_ge(S[f"acc_out{h}"], 16 + 16 * k)
                        V.scalar_tensor_tensor(out=av, in0=acc_old[h][:, 0:D], scalar=later[0:P, bass.ds(r, 1)],
                                               in1=ps_a[h][0:P, 0:D], op0=ALU.mult, op1=ALU.add) \
                            .then_inc(S[f"acc_made{h}"], 1)
                        dve.wait_ge(S[f"acc_made{h}"], UP + k + 1)
                        dve.wait_ge(S[f"f2_made{h}"], j + 1)
                        V.scalar_tensor_tensor(out=U[h][:], in0=av, scalar=rso[:, col], in1=F[h][:],
                                               op0=ALU.mult, op1=ALU.add).then_inc(S["up_made"], 1)
                        V.scalar_tensor_tensor(out=F[h][:], in0=av, scalar=rso[:, col], in1=F[h][:],
                                               op0=ALU.mult, op1=ALU.mult).then_inc(S["up_made"], 1)
                        dve.wait_ge(S["o_ps"], i + 1)
                        dve.wait_ge(S[f"y_out{h}"], 16 + 16 * j)
                        own(V.scalar_tensor_tensor(out=y[h][:], in0=ps_o[0:P, 0:D], scalar=filled[:, col], in1=b1_s[:],
                                                   op0=ALU.mult, op1=ALU.add))
                        dve.sem_inc(S["o_read"], 1)
                        own(V.scalar_tensor_tensor(out=y[h][:], in0=y[h][:], scalar=0.01, in1=y[h][:],
                                                   op0=ALU.mult, op1=ALU.max))
                        V.tensor_tensor_reduce(out=junk[:], in0=y[h][:], in1=y[h][:], scale=1.0, scalar=0.0,
                                               op0=ALU.mult, op1=ALU.add, accum_out=sm[:, 0:1]).then_inc(S["ss_made"], 1)
                        dve.wait_ge(S["norm_made"], i + 1)
                        own(V.tensor_scalar(sm[:, 1:2], sm[:, 2:3], 1e-12, None, ALU.max))
                        own(V.reciprocal(sm[:, 3:4], sm[:, 1:2]))
                        dve.wait_ge(S[f"x1_in{h}"], 16 * (j + 1))
                        own(V.scalar_tensor_tensor(out=y[h][:], in0=y[h][:], scalar=sm[:, 3:4], in1=xt[h][:],
                                                   op0=ALU.mult, op1=ALU.add))
                        dve.sem_inc(S[f"y_made{h}"], 1)
                        assert made[0] == n_own, made[0]

        @block.scalar
        def _(act):
            A = nc.scalar
            for w_s, w_d in ((Wv_s, Wv), (W1_s, W1), (W2_s, W2)):
                act.dma_start(w_s[:], w_d.rearrange("(c p) n -> p c n", p=128)).then_inc(S["consts_in"], 16)
            for r_s, r_d in ((bv_s, bv), (wq_s, wq), (wk_s, wk), (b1_s, b1)):
                act.dma_start(r_s[:], r_d.unsqueeze(0).to_broadcast([P, D])).then_inc(S["consts_in"], 16)
            for c, s_d in enumerate((bq, bk)):
                act.dma_start(bqk[:, c:c + 1], s_d.unsqueeze(0).to_broadcast([P, 1])).then_inc(S["consts_in"], 16)
            for n, name in enumerate(stores):
                act.dma_start(primed[:, n:n + 1], bq.unsqueeze(0)).then_inc(S[name], 16)
            act.wait_ge(S["pre_std"], 1)
            A.activation(rstd[:], nmr[:], ACT.Sqrt).then_inc(S["pre_rstd"], 1)
            act.wait_ge(S["pre_scaled"], 1)
            def normalized(t):
                if t >= 2:
                    act.wait_ge(S["hn_T"], t - 1)
                A.activation(hn[t % 2][:], xs[t // XH][:, t % XH, :], ACT.Relu, bias=nmr[:, t:t + 1],
                             scale=rstd[:, t:t + 1]).then_inc(S["hn_made"], 1)

            normalized(0)
            for t in range(NB):
                if t + 1 < NB:
                    normalized(t + 1)
                act.wait_ge(S["hn_T"], t + 1)
                if t >= 2:
                    act.wait_ge(S["h_ps"], t - 1)
                A.activation(hT[t % 2][:, 0:2, :], ps_tt[t % 2][:, 0:2, 0:P], ACT.Copy).then_inc(S["hT_made"], 1)
            act.wait_ge(S["windows_out"], 16)
            R = rounds(act)

            def weights(b, k, h):
                i = 2 * k + h
                act.wait_ge(S[f"ndl_made{h}"], UP + k + 1)
                act.wait_ge(S[f"used{h}1"], UP + k)
                for t in range(T):
                    last = A.activation(wts[h][:, t, :], slot[:, 0:P], ACT.Square, bias=ndl[h][:, t:t + 1])
                last.then_inc(S[f"sq_made{h}"], 1)
                act.wait_ge(S["corr_in"], i + 1)
                A.activation(corr[h][:, 1:2], corr[h][:, 0:1], ACT.Exp).then_inc(S["corr_made"], 1)
                act.wait_ge(S["lw_made"], i + 1)
                for t in range(T):
                    last = A.activation(wts[h][:, t, :], wts[h][:, t, :], ACT.Exp, bias=ew[h][:, 5, t:t + 1])
                    if t % TC == TC - 1:
                        last.then_inc(S[f"w_made{h}{t // TC}"], 1)

            def normalize(b, k, h):
                i, col = 2 * k + h, bass.ds(b, 1)
                act.wait_ge(S["std1_in"], i + 1)
                A.activation(sf[:, 3:4], sf[:, 2:3], ACT.Sqrt).then_inc(S["std1_made"], 1)
                act.wait_ge(S["scaled1"], i + 1)
                act.wait_ge(S[f"f_out{h}"], 16 + 16 * k)
                A.activation(trow[h][:, 0:D], x1t[h][:], ACT.Relu, bias=nmr1[:, col],
                             scale=rstd1[:, col]).then_inc(S[f"f_made{h}"], 1)
                rows_of = bass.ds(b * P, P)
                act.dma_start(accd[rows_of, :], acc_new[h][:]).then_inc(S[f"acc_out{h}"], 16)
                act.dma_start(x1d[rows_of, :], x1t[h][:]).then_inc(S[f"x1_out{h}"], 16)
                act.wait_ge(S[f"f_made{h}"], UP + k + 1)
                act.dma_start(tab1[rows_of, :], trow[h][:]).then_inc(S[f"f_out{h}"], 16)

            with act.Fori(0, R) as r:
                weights(0, r * XH, 0)
                with act.Fori(0, XH - 1) as p:
                    k = r * XH + p
                    weights(2 * p + 1, k, 1)
                    normalize(2 * p, k, 0)
                    weights(2 * p + 2, k + 1, 0)
                    normalize(2 * p + 1, k, 1)
                weights(NB - 1, r * XH + XH - 1, 1)
                normalize(NB - 2, r * XH + XH - 1, 0)
                normalize(NB - 1, r * XH + XH - 1, 1)
            act.wait_ge(S["deg_made"], 1)
            A.activation(sod[:], outdeg[:], ACT.Sqrt).then_inc(S["sod_made"], 1)
            with act.Fori(0, R) as r:
                with act.Fori(0, XH) as p:
                    j = r * XH + p
                    for h in range(2):
                        i, b = 2 * j + h, 2 * p + h
                        col = bass.ds(b, 1)
                        act.wait_ge(S[f"x1_in{h}"], 16 * (j + 1))
                        act.wait_ge(S["upT_made"], UP + i)
                        A.activation(F[h][:], xt[h][:], ACT.Relu, bias=nmr1[:, col],
                                     scale=rstd1[:, col]).then_inc(S[f"f2_made{h}"], 1)
                        act.wait_ge(S["upT_made"], UP + i + 1)
                        A.activation(hT[h][:], ps_t[:, :, 0:P], ACT.Copy).then_inc(S["upT_copied"], 1)
                        act.wait_ge(S[f"acc_made{h}"], UP + j + R * XH + 1)
                        act.dma_start(accd[bass.ds(b * P, P), :], acc_new[h][:]).then_inc(S[f"acc_out{h}"], 16)
                        act.wait_ge(S["ss_made"], i + 1)
                        A.activation(sm[:, 2:3], sm[:, 0:1], ACT.Sqrt).then_inc(S["norm_made"], 1)
                        act.wait_ge(S[f"y_made{h}"], UP + j + 1)
                        act.dma_start(out[bass.ds(b * P, P), :], y[h][:]).then_inc(S[f"y_out{h}"], 16)

        @block.tensor
        def _(pe):
            TE = nc.tensor
            for name in counters:
                pe.sem_inc(S[name], UP)
            pe.wait_ge(S["dve_iota"], 1)
            pe.wait_ge(S["consts_in"], 9 * 16)

            def turn(t, h, before):
                pe.wait_ge(S["hn_made"], t + 1)
                pe.wait_ge(S["hT_made"], before)
                for c in range(2):
                    last = TE.transpose(ps_tt[h][:, c, 0:P], hn[h][:, c * 128:(c + 1) * 128], ident[0:P, 0:P])
                last.then_inc(S["hn_T"], 1)

            def project(t, h, read):
                pe.wait_ge(S["hT_made"], UP + t + 1)
                pe.wait_ge(S["h_row"], read)
                for c in range(2):
                    last = TE.matmul(ps_a[h][0:P, 0:D], hT[h][:, c, :], Wv_s[:, c, :], start=(c == 0), stop=(c == 1))
                last.then_inc(S["h_ps"], 1)

            turn(0, 0, UP)
            turn(1, 1, UP)
            project(0, 0, UP)
            with pe.Fori(0, XH - 1) as p:
                turn(2 * p + 2, 0, UP + 2 * p + 1)
                project(2 * p + 1, 1, 2 * p + UP)
                turn(2 * p + 3, 1, UP + 2 * p + 2)
                project(2 * p + 2, 0, 2 * p + 1 + UP)
            project(NB - 1, 1, NB - 2 + UP)
            pe.wait_ge(S["windows_made"], 1)
            pe.wait_ge(S["k3_made"], 1)
            pe.wait_ge(S["h_row"], UP + NB)
            R = rounds(pe)

            def sums(h, k, width):
                for c in range(2):
                    pe.wait_ge(S[f"w_made{h}{c}"], UP + k + 1)
                    for t in range(c * TC, (c + 1) * TC):
                        last = TE.matmul(ps_a[h][0:P, 0:width], wts[h][:, t, :], rows[h][:, t, 0:width],
                                         start=(t == 0), stop=(t == T - 1))
                    last.then_inc(S[f"used{h}{c}"], 1)

            with pe.Fori(0, R) as r:
                with pe.Fori(0, XH) as p:
                    k = r * XH + p
                    for h in range(2):
                        i = 2 * k + h
                        one_hots = dT[h][:].bitcast(bf16).rearrange("s (e t) -> s t e", t=T)
                        pe.wait_ge(S["ohT_made"], i + 1)
                        pe.wait_ge(S["me_made"], UP + i)
                        for t in range(T):
                            last = TE.matmul(ps_k[:, 3 * t:3 * t + 3], one_hots[:, t, :], k3[:, bass.ds(2 * p + h, 1), :]
                                             .rearrange("s a c -> s (a c)"), start=True, stop=True)
                        last.then_inc(S["ke_made"], 1)
                        pe.wait_ge(S["half_max"], i + 1)
                        TE.transpose(ps_q[0:P, 0:128], qm[:, 2, :], ident[:]).then_inc(S["qT_made"], 1)
                        pe.wait_ge(S["m3_made"], i + 1)
                        for t in range(T):
                            last = TE.matmul(ps_m[:, 3 * t:3 * t + 3], one_hots[:, t, :], m3[:], start=True, stop=True)
                        last.then_inc(S["me_made"], 1)
                        sums(h, k, D + 1)
                        pe.wait_ge(S["oh_made"], 2 * i + 2)
                        pe.wait_ge(S["hist_made"], UP + i)
                        for t in range(HT):
                            last = TE.matmul(ps_h[0:P, 0:NB], oh_lo[:, t, :], oh_hi[:, t, :], start=(t == 0), stop=(t == HT - 1))
                        last.then_inc(S["hist_ps"], 1)
            with pe.Fori(0, R) as r:
                with pe.Fori(0, XH) as p:
                    j = r * XH + p
                    k = j + R * XH
                    for h in range(2):
                        i = 2 * j + h
                        sums(h, k, D)
                        pe.wait_ge(S["up_made"], 2 * i + 2)
                        pe.wait_ge(S["upT_copied"], UP + i)
                        for c in range(4):
                            m = (U, F)[c // 2][h]
                            last = TE.transpose(ps_t[:, c, 0:P], m[:, c % 2 * 128:(c % 2 + 1) * 128], ident[0:P, 0:P])
                        last.then_inc(S["upT_made"], 1)
                        pe.wait_ge(S["upT_copied"], UP + i + 1)
                        pe.wait_ge(S["o_read"], UP + i)
                        for c in range(4):
                            last = TE.matmul(ps_o[0:P, 0:D], hT[h][:, c, :], (W1_s, W2_s)[c // 2][:, c % 2, :],
                                             start=(c == 0), stop=(c == 3))
                        last.then_inc(S["o_ps"], 1)


_INS = ["x", "src", "dst", "L0_gnn_Wv", "L0_gnn_bv", "L0_gnn_wq", "L0_gnn_bq", "L0_gnn_wk", "L0_gnn_bk",
        "L1_gnn_W1", "L1_gnn_W2", "L1_gnn_b"]


def kernel(**inputs):
    import numpy as _np
    import concourse.bacc as _bacc
    from concourse import mybir as _mybir
    from concourse.bass_utils import run_bass_kernel_spmd as _run

    nc = _bacc.Bacc("TRN2", target_bir_lowering=False, num_devices=1)
    arrays, args = {}, []
    for name in _INS:
        a = _np.ascontiguousarray(inputs[name])
        if a.ndim == 0:
            a = a.reshape(1)
        arrays[f"in_{name}"] = a
        args.append(nc.dram_tensor(f"in_{name}", a.shape, _mybir.dt.from_np(a.dtype), kind="ExternalInput").ap())
    args.append(nc.dram_tensor("out_0", (N, D), _mybir.dt.float32, kind="ExternalOutput").ap())
    gnn(nc, *args)
    r = _run(nc, [arrays], core_ids=[0])
    return r.results[0]["out_0"]
```

```python
import concourse.bass as bass
from concourse import mybir
from contextlib import ExitStack

N, D, E = 6250, 256, 200000
P = 125
NB = N // P
T = 34
TC = T // 2
TT = 27
TF = 4
WIN = T * 128
RMAX = -(-E // WIN)
TW = 260
ONE, QC, RS = D, D + 1, D
EC = E // P
G = 5
NG, GB = N // G, P // G
WG = 256
GC = 5
NC = GB // GC
KEYS = G * NB
FG = 5
SPL = 160
NS = E // SPL
HT = EC // NB
SCALE = 2.0 ** 47
SLOTS = (0, 1, 2, 0, 1)
NR = 3
HC = 500
NODST = 7000.0
UP = 1
MAGIC = 12582912.0


def gnn(nc, x, src, dst, Wv, bv, wq, bq, wk, bk, W1, W2, b1, out):
    f32, bf16, i32, u32, u8 = mybir.dt.float32, mybir.dt.bfloat16, mybir.dt.int32, mybir.dt.uint32, mybir.dt.uint8
    i16 = mybir.dt.int16
    ALU, ACT, AX = mybir.AluOpType, mybir.ActivationFunctionType, mybir.AxisListType

    edges = nc.dram_tensor("edges", (E + WIN, 2), i32).ap()
    dst16 = nc.dram_tensor("dst16", (E + WIN,), i16).ap()
    accd = nc.dram_tensor("accd", (N, D + 1), f32).ap()
    startd = nc.dram_tensor("startd", (NG,), f32).ap()
    keyd = nc.dram_tensor("keyd", (E + WIN, 2), f32).ap()
    countd = nc.dram_tensor("countd", (NB, P, P * NB), bf16).ap()
    wind = nc.dram_tensor("wind", (1, RMAX * NB), i32).ap()
    tab0 = nc.dram_tensor("tab0", (N, TW), f32).ap()
    tab1 = nc.dram_tensor("tab1", (N, TW), f32).ap()
    x1d = nc.dram_tensor("x1d", (N, D), f32).ap()

    ctx = ExitStack()
    with ctx:
        def sb(name, shape, dt=f32):
            return ctx.enter_context(nc.sbuf_tensor(name, shape, dt))

        def pb(name, shape, dt=f32):
            return ctx.enter_context(nc.psum_tensor(name, shape, dt))

        def sem(name):
            return ctx.enter_context(nc.semaphore(name))

        ROWS, WTS = T * TW, T * P
        arena = sb("arena", [128, 2 * ROWS + 2 * WTS])
        rows = [arena[:, h * ROWS:(h + 1) * ROWS].rearrange("p (t c) -> p t c", c=TW) for h in range(2)]
        wts = [arena[:, 2 * ROWS + h * WTS:2 * ROWS + (h + 1) * WTS].rearrange("p (t s) -> p t s", s=P)
               for h in range(2)]
        acc_old = [sb(f"acc_old{h}", [P, D + 1]) for h in range(2)]
        acc_new = [sb(f"acc_new{h}", [P, D + 1]) for h in range(2)]
        dT = sb("dT", [P, WIN], i16)
        count = sb("count", [P, P * NB], bf16)
        oh_key = sb("oh_key", [128, NR * GC * 2 * KEYS], bf16)
        oh_low = sb("oh_low", [128, NR * GC * 2 * P], bf16)
        keys = sb("keys", [128, 4, NG], bf16)
        kb = sb("kb", [128, 2, GB])
        iota_kb = sb("iota_kb", [128, KEYS], bf16)
        iota_ki = sb("iota_ki", [128, KEYS], i32)
        thc_i = sb("thc_i", [P, NG // P], i32)
        thc = sb("thc", [P, NG // P])
        gneg = sb("gneg", [P, NG // P])
        one_b = sb("one_b", [P, 1], bf16)
        gs = sb("gs", [P, 5, NG // P])
        gs_i = sb("gs_i", [P, 2, NG // P], u32)
        node_i = sb("node_i", [P, NB], i32)
        node = sb("node", [P, NB])
        k3 = sb("k3", [P, NB, 3], bf16)
        k_rest = sb("k_rest", [P, NB])
        m3 = sb("m3", [P, 3], bf16)
        ew = [sb(f"ew{h}", [128, 6, T]) for h in range(2)]
        pad16 = sb("pad16", [128, T], i16)
        edge = [sb(f"edge{h}", [128, T, 2], i32) for h in range(2)]
        ndl = [sb(f"ndl{h}", [128, T]) for h in range(2)]
        ident_b = sb("ident_b", [P, P], bf16)
        zero_b = sb("zero_b", [P, P], bf16)
        slot_i = sb("slot_i", [128, 128], i32)
        slot = sb("slot", [128, 128])
        slot_b = sb("slot_b", [128, 128], bf16)
        part_i = sb("part_i", [128, 1], i32)
        part = sb("part", [128, 1])
        ident = sb("ident", [128, 128])
        base_i = sb("base_i", [128, NB], i32)
        base = sb("base", [128, NB])
        base_s = sb("base_s", [128, NB])
        first = sb("first", [128, RMAX + 1])
        later = sb("later", [128, RMAX + 1])
        rstep_i = sb("rstep_i", [1, RMAX + 1], i32)
        rstep = sb("rstep", [1, RMAX + 1])
        Wv_s = sb("Wv_s", [128, 2, D])
        W1_s = sb("W1_s", [128, 2, D])
        W2_s = sb("W2_s", [128, 2, D])
        bv_s, wq_s, wk_s, b1_s = (sb(n, [P, D]) for n in ("bv_s", "wq_s", "wk_s", "b1_s"))
        primed = sb("primed", [1, 12])
        bqk = sb("bqk", [P, 2])
        mv = sb("mv", [P, NB, 2])
        rstd = sb("rstd", [P, NB])
        nmr = sb("nmr", [P, NB])
        rstd1 = sb("rstd1", [P, NB])
        nmr1 = sb("nmr1", [P, NB])
        kcol = sb("kcol", [P, NB])
        mcol = sb("mcol", [P, NB])
        outdeg = sb("outdeg", [P, NB])
        sod = sb("sod", [P, NB])
        rso = sb("rso", [P, NB])
        filled = sb("filled", [P, NB])
        stats = sb("stats", [P, NB, 6])
        hn = [sb(f"hn{h}", [P, D]) for h in range(2)]
        hT = [sb(f"hT{h}", [128, 4, P]) for h in range(2)]
        trow = [sb(f"trow{h}", [P, TW]) for h in range(2)]
        junk = sb("junk", [P, D])
        xt = [sb(f"xt{h}", [P, D]) for h in range(2)]
        x1t = [sb(f"x1t{h}", [P, D]) for h in range(2)]
        U, F = x1t, hn
        y = [sb(f"y{h}", [P, D]) for h in range(2)]
        qm = sb("qm", [128, 3, P])
        sc = sb("sc", [P, 8])
        corr = [sb(f"corr{h}", [P, 2]) for h in range(2)]
        sf = sb("sf", [P, 6])
        sm = sb("sm", [P, 4])
        spl_s = sb("spl_s", [P, EC // SPL])
        gap = sb("gap", [1, NB])
        rnd_f = sb("rnd_f", [1, RMAX + 4])
        flags = sb("flags", [1, 8])
        rnd = sb("rnd", [1, 4], i32)
        padi = sb("padi", [128, T, 2], i32)
        padk = sb("padk", [128, T, 2])

        def piece(at, n, dt=f32, parts=P):
            return arena[0:parts, at:at + n].bitcast(dt) if dt != f32 else arena[0:parts, at:at + n]

        W0 = 2 * ROWS
        win = piece(W0 + WTS, RMAX * NB, i32, 1)
        srcs, dsts = piece(W0, EC, i32), piece(W0 + EC, EC, i32)
        pairs = piece(W0 + WTS, 2 * EC, i32).rearrange("p (e c) -> p e c", c=2)
        XH = NB // 2
        xs = [piece(h * XH * D, XH * D).rearrange("p (t d) -> p t d", d=D) for h in range(2)]
        tmp_hi = piece(NB * D, EC)
        key_pairs = piece(NB * D + EC, 2 * EC).rearrange("p (e c) -> p e c", c=2)
        NSP = EC // SPL
        below = [count[:, c * NG:(c + 1) * NG] for c in range(5)] \
            + [dT[:, c * NG:(c + 1) * NG].bitcast(bf16) for c in range(3)] \
            + [oh_key[0:P, c * NG:(c + 1) * NG] for c in range(2)]
        group_row = oh_key[0:P, 2 * NG:4 * NG].bitcast(i32)
        d16 = oh_low[0:P, 0:EC].bitcast(i16)
        found = count[:, 0:2 * NSP * SPL].bitcast(i32).rearrange("p (j e) -> p j e", e=SPL)
        found_f = count[:, 0:2 * NSP * SPL].bitcast(f32).rearrange("p (j e) -> p j e", e=SPL)
        st_row = dT[0:1, 0:2 * (NG + 1)].bitcast(f32)
        steps_row = count[0:1, 0:2 * NG].bitcast(f32)
        wedge_at = [piece(NB * D + j * 2 * WG, 2 * WG) for j in range(9)] + [oh_low[0:P, 0:4 * WG].bitcast(f32)]
        wedge = [w.rearrange("p (e c) -> p e c", c=2) for w in wedge_at]
        assert NB * D + 3 * EC <= 2 * ROWS
        g_src = piece(0, EC, i32)
        g_hi, g_lo = piece(EC, EC), piece(2 * EC, EC)
        oh_lo = piece(3 * EC, HT * P // 2, bf16).rearrange("p (t s) -> p t s", s=P)
        oh_hi = piece(3 * EC + HT * P // 2, HT * NB // 2, bf16).rearrange("p (t s) -> p t s", s=NB)
        split = piece(0, NB * 3 * D // 2, bf16).rearrange("p (t c) -> p t c", c=3 * D)
        CW = P * NB // 2
        counts = [piece(NB * 3 * D // 2 + h * CW, CW, bf16).rearrange("p (s u) -> p u s", u=NB) for h in range(2)]
        assert NB * 3 * D // 2 + 2 * CW <= 2 * ROWS + 2 * WTS
        f_in = [count[:, h * 2 * FG * D:(h + 1) * 2 * FG * D].bitcast(f32).rearrange("p (t d) -> p t d", d=D)
                for h in range(2)]
        rest = [t[0:P, 0:2 * FG * D].bitcast(f32).rearrange("p (t d) -> p t d", d=D) for t in (dT, oh_key)]

        ps_q = pb("ps_q", [128, 512])
        ps_k = pb("ps_k", [128, 512])
        ps_m = pb("ps_m", [128, 512])
        ps_h = pb("ps_h", [128, 512])
        ps_a = [pb(f"ps_a{h}", [128, 512]) for h in range(2)]
        ps_t = pb("ps_t", [128, 4, 128])
        ps_o = pb("ps_o", [128, 512])
        ps_key = [ps[:].rearrange("p (c n) -> p c n", n=128)[:, :, 0:P] for ps in (ps_k, ps_h)]
        ps_ct = [ps_t[:].rearrange("p a b -> p (a b)")[0:P, 0:2 * KEYS], ps_o[0:P, 0:2 * KEYS]]
        ps_tt = [ps_t[:], ps_o[:].rearrange("p (c n) -> p c n", n=128)]

        names = """edges_in consts_in x_in0 x_in1 iotas dve_iota pairs_made pairs_out pads_made
            split_made compared counted gst_made key_out wedge_in key_made keyT keys_made ring_full
            ring_used ct_ps ct_copied ct_out0 ct_out1 deg_part deg_ps deg_read g_src_in dve_g v_made
            w_first0 w_first1 g_x1_in0 g_x1_in1 ct_in0 ct_in1 fin0 fin1 a_made r_made b_made c_made d_sum0
            d_sum1 chunk_at chunk_in start_made start_out start_in windows_made windows_out lohi pre_std
            pre_rstd pre_scaled hn_made hn_T hT_made h_ps h_row pre_tab0 pre_tab1 edge_in0 edge_in1
            ndl_made0 ndl_made1 sq_made0 sq_made1 got00 got01 got10 got11 used00 used01 used10 used11
            half_max qT_made m3_made ke_made me_made ohT_made dst16_out zero_out dT_in acc_in0 acc_in1
            acc_out0 acc_out1 acc_made0 acc_made1 lw_made w_read k3_made dve_f w_made00 w_made01 w_made10
            w_made11 corr_in corr_made oh_made hist_ps hist_made x_in_l0 x_in_l1 x1_made0 x1_made1 f_made0
            f_made1 f_out0 f_out1 x1_out0 x1_out1 deg_made sod_made rs_made rs_out x1_in0 x1_in1 f2_made0
            f2_made1 up_made upT_made upT_copied o_ps o_read ss_made norm_made y_out0 y_out1 y_made0 y_made1
            settled dve_c pool_c fin_used""".split()
        S = {n: sem(n) for n in names}
        counters = """used00 used01 used10 used11 ndl_made0 ndl_made1 x1_made0 x1_made1 f_made0 f_made1
            hist_ps hist_made y_made0 y_made1 upT_made upT_copied o_read hT_made h_row
            w_made00 w_made01 w_made10 w_made11 acc_made0 acc_made1 me_made ring_full d_sum0 d_sum1 ring_used ct_copied
            up_made up_made c_made c_made b_made fin_used fin_used w_first0 w_first1 ring_used ring_used ct_copied deg_part deg_part""".split()
        stores = "x1_out0 x1_out1 f_out0 f_out1 y_out0 y_out1 pre_tab0 pre_tab1 acc_out0 acc_out1 ct_out0 ct_out1".split()

        def over_tiles(col, n, w):
            return col.unsqueeze(1).to_broadcast([col.shape[0], n, w])

        def over_slots(col, n, w):
            return col.unsqueeze(2).to_broadcast([col.shape[0], n, w])

        def v_bank(h, c, u):
            return (h + c + u) % 2

        def settle(eng):
            eng.sem_inc(S["settled"], 1)

        def rounds(eng):
            return [eng.value_load(rnd[0:1, n:n + 1], min_val=int(n == 0), max_val=(RMAX, 1, RMAX, 1)[n])
                    for n in range(4)]

        block = ctx.enter_context(nc.Block())

        @block.sync
        def _(sp):
            sp.dma_start(dsts, dst.rearrange("(p e) -> p e", p=P)).then_inc(S["edges_in"], 16)
            sp.dma_start(srcs, src.rearrange("(p e) -> p e", p=P)).then_inc(S["edges_in"], 16)
            xv = x.rearrange("(t p) d -> p t d", p=P)
            for h in range(2):
                sp.dma_start(xs[h], xv[:, h * XH:(h + 1) * XH, :]).then_inc(S[f"x_in{h}"], 16)
            sp.wait_ge(S["pairs_made"], 1)
            sp.dma_start(edges[0:E, :].rearrange("(p e) c -> p e c", p=P), pairs).then_inc(S["pairs_out"], 16)
            sp.wait_ge(S["pads_made"], 1)
            sp.dma_start(edges[E:E + WIN, :].rearrange("(p e) c -> p e c", p=128), padi[:]).then_inc(S["pairs_out"], 16)
            sp.wait_ge(S["split_made"], 2)
            sp.dma_start(dst16[0:E].rearrange("(p e) -> p e", p=P), d16).then_inc(S["dst16_out"], 16)
            sp.dma_start(dst16[E:E + WIN].rearrange("(p e) -> p e", p=128), pad16[:]).then_inc(S["dst16_out"], 16)
            sp.wait_ge(S["lohi"], 3)
            sp.dma_start(keyd[0:E, :].rearrange("(p e) c -> p e c", p=P), key_pairs).then_inc(S["key_out"], 16)
            sp.dma_start(keyd[E:E + WIN, :].rearrange("(p e) c -> p e c", p=128), padk[:]).then_inc(S["key_out"], 16)
            sp.dma_start(accd.rearrange("(t p) c -> p t c", p=P), over_tiles(acc_new[0][:], NB, D + 1)) \
                .then_inc(S["zero_out"], 16)
            sp.wait_ge(S["start_made"], 1)
            with nc.allow_non_contiguous_dma(reason="group starts"):
                sp.dma_start(startd.rearrange("(j p) -> p j", p=P), gs[:, 4, :]).then_inc(S["start_out"], 16)
            sp.wait_ge(S["start_out"], 16)
            sp.dma_start(st_row[:, 0:NG], startd.unsqueeze(0)).then_inc(S["start_in"], 16)
            sp.wait_ge(S["pairs_out"], 32)
            sp.wait_ge(S["windows_made"], 1)
            sp.dma_start(wind, win).then_inc(S["windows_out"], 16)
            with sp.Fori(0, XH) as p:
                for h in range(2):
                    sp.wait_ge(S["h_row"], UP + 2 * p + h + 1)
                    sp.dma_start(tab0[bass.ds((2 * p + h) * P, P), :], trow[h][:]).then_inc(S[f"pre_tab{h}"], 16)
            sp.wait_ge(S["windows_out"], 16)
            R, RD, RG, G1 = rounds(sp)
            for h in range(2):
                sp.wait_ge(S[f"pre_tab{h}"], 16 + 16 * XH)
            sp.wait_ge(S["keyT"], NG // P)
            sp.wait_ge(S["dst16_out"], 32)
            sp.wait_ge(S["zero_out"], 16)

            def window(r, b, k, h, weighed):
                e0 = sp.value_load(wind[0:1, bass.ds(r * NB + b, 1)], min_val=0, max_val=E)
                sp.wait_ge(S[weighed], UP + k)
                sp.dma_start(edge[h][:], edges[bass.ds(e0, WIN), :].rearrange("(p e) c -> p e c", p=128)) \
                    .then_inc(S[f"edge_in{h}"], 16)
                return e0

            def sums_so_far(b, k, h):
                sp.wait_ge(S[f"acc_made{h}"], UP + k)
                settle(sp)
                sp.wait_ge(S[f"acc_out{h}"], 16 + 16 * k)
                sp.dma_start(acc_old[h][:], accd[bass.ds(b * P, P), :]).then_inc(S[f"acc_in{h}"], 16)

            def head(r, b, k, h):
                e0 = window(r, b, k, h, f"w_first{h}")
                sp.wait_ge(S["me_made"], UP + 2 * k + h)
                sp.dma_start(dT[:], dst16[bass.ds(e0, WIN)].unsqueeze(0).to_broadcast([P, WIN])) \
                    .then_inc(S["dT_in"], 16)

            def tail(b, k, h):
                sp.wait_ge(S[f"x1_made{h}"], UP + k)
                sp.dma_start(xt[h][:], x[bass.ds(b * P, P), :]).then_inc(S[f"x_in_l{h}"], 16)
                sums_so_far(b, k, h)

            with sp.Fori(0, R) as r:
                k = r * XH
                head(r, 0, k, 0)
                head(r, 1, k, 1)
                tail(0, k, 0)
                with sp.Fori(0, XH - 1) as p:
                    k = r * XH + p
                    head(r, 2 * p + 2, k + 1, 0)
                    tail(2 * p + 1, k, 1)
                    head(r, 2 * p + 3, k + 1, 1)
                    tail(2 * p + 2, k + 1, 0)
                tail(NB - 1, r * XH + XH - 1, 1)
            KR = R * XH
            for h in range(2):
                sp.wait_ge(S[f"x1_out{h}"], 16 + KR * 16)
                settle(sp)
            for h in range(2):
                sp.wait_ge(S[f"ct_out{h}"], 16 + 16 * R * NB)
                settle(sp)
            sp.wait_ge(S["deg_ps"], R)
            settle(sp)
            with sp.If(RD > 0):
                x1_v = x1d.rearrange("(t p) c -> p t c", p=P)
                with sp.Fori(0, NB // FG // 2) as g:
                    for h in range(2):
                        sp.wait_ge(S["fin_used"], 2 * g + h + 1)
                        sp.dma_start(f_in[h], x1_v[:, bass.ds((2 * g + h) * FG, FG), :]).then_inc(S[f"fin{h}"], 16)
                for h in range(2):
                    sp.wait_ge(S[f"used{h}1"], UP + KR)
                    settle(sp)
                with sp.Fori(0, XH) as p:
                    for h in range(2):
                        sp.wait_ge(S[f"d_sum{h}"], UP + p)
                        sp.dma_start(counts[h].rearrange("p u s -> p s u").rearrange("p s u -> p (s u)"),
                                     countd[bass.ds(2 * p + h, 1), :, :].rearrange("a p c -> p (a c)")) \
                            .then_inc(S[f"ct_in{h}"], 16)
                        sp.wait_ge(S[f"y_made{h}"], UP + p)
                        sp.dma_start(xt[h][:], x1d[bass.ds((2 * p + h) * P, P), :]).then_inc(S[f"x1_in{h}"], 16)
            with sp.If(G1 > 0):
                for h in range(2):
                    sp.wait_ge(S[f"used{h}1"], UP + KR)
                    settle(sp)
                sp.dma_start(g_src, src.rearrange("(p e) -> p e", p=P)).then_inc(S["g_src_in"], 16)
                for h in range(2):
                    sp.wait_ge(S[f"x1_made{h}"], UP + KR)
                    settle(sp)
                with sp.Fori(0, XH) as p:
                    for h in range(2):
                        sp.wait_ge(S[f"f_made{h}"], UP + p)
                        sp.dma_start(xt[h][:], x1d[bass.ds((2 * p + h) * P, P), :]).then_inc(S[f"g_x1_in{h}"], 16)
                for h in range(2):
                    sp.wait_ge(S[f"f_out{h}"], 16 + 16 * XH)
                sp.wait_ge(S["rs_made"], 5)
                with nc.allow_non_contiguous_dma(reason="one column of the table"):
                    sp.dma_start(tab1.rearrange("(t p) c -> p t c", p=P)[:, :, RS:RS + 1], rso[:].unsqueeze(2)) \
                        .then_inc(S["rs_out"], 16)
            with sp.If(G1 > 0), sp.Fori(0, RG) as r:
                with sp.Fori(0, XH) as p:
                    k = r * XH + p + KR
                    for h in range(2):
                        window(r, 2 * p + h, k, h, f"w_made{h}1")
                        sp.wait_ge(S[f"y_made{h}"], UP + r * XH + p)
                        sp.dma_start(xt[h][:], x1d[bass.ds((2 * p + h) * P, P), :]).then_inc(S[f"x1_in{h}"], 16)
                        sums_so_far(2 * p + h, k, h)
            for h in range(2):
                sp.wait_ge(S[f"f_out{h}"], 16)
                sp.wait_ge(S[f"y_out{h}"], 16 + (RD + RG) * XH * 16)
                sp.wait_ge(S[f"acc_out{h}"], 16 + (R + RG) * XH * 16)
            settle(sp)

        @block.gpsimd
        def _(pool):
            nc.gpsimd.iota(slot_i[:], [[1, 128]], base=0, channel_multiplier=0).then_inc(S["iotas"], 1)
            nc.gpsimd.iota(part_i[:], [[0, 1]], base=0, channel_multiplier=1).then_inc(S["iotas"], 1)
            nc.gpsimd.iota(base_i[:], [[P, NB]], base=0, channel_multiplier=0).then_inc(S["iotas"], 1)
            nc.gpsimd.iota(rstep_i[:], [[WIN, RMAX + 1]], base=0, channel_multiplier=0).then_inc(S["iotas"], 1)
            nc.gpsimd.memset(acc_new[0][:], 0.0).then_inc(S["iotas"], 1)
            nc.gpsimd.iota(node_i[:], [[P, NB]], base=0, channel_multiplier=1).then_inc(S["iotas"], 1)
            nc.gpsimd.memset(later[:, 0:1], 0.0).then_inc(S["iotas"], 1)
            nc.gpsimd.memset(later[:, 1:RMAX + 1], 1.0).then_inc(S["iotas"], 1)
            nc.gpsimd.iota(iota_ki[:], [[1, KEYS]], base=0, channel_multiplier=0).then_inc(S["iotas"], 1)
            nc.gpsimd.iota(thc_i[:], [[G * P, NG // P]], base=0, channel_multiplier=G).then_inc(S["iotas"], 1)
            nc.gpsimd.memset(one_b[:], 1.0).then_inc(S["iotas"], 1)
            nc.gpsimd.memset(first[:, 0:1], 1.0).then_inc(S["iotas"], 1)
            nc.gpsimd.memset(first[:, 1:RMAX + 1], 0.0).then_inc(S["iotas"], 1)
            nc.gpsimd.memset(zero_b[:], 0.0).then_inc(S["iotas"], 1)
            nc.gpsimd.memset(mcol[:], -1e30).then_inc(S["iotas"], 1)
            for h in range(2):
                nc.gpsimd.memset(trow[h][:, D:TW], 0.0).then_inc(S["pool_c"], 1)
                pool.wait_ge(S["pool_c"], h + 1)
                nc.gpsimd.memset(trow[h][:, ONE:ONE + 1], 1.0).then_inc(S["iotas"], 1)
            nc.gpsimd.memset(padi[:, :, 0:1], 0).then_inc(S["pool_c"], 1)
            nc.gpsimd.memset(padi[:, :, 1:2].bitcast(f32), NODST).then_inc(S["pool_c"], 1)
            nc.gpsimd.memset(padk[:, :, 0:1], 0.0).then_inc(S["pool_c"], 1)
            nc.gpsimd.memset(padk[:, :, 1:2], NB * NODST).then_inc(S["pool_c"], 1)
            nc.gpsimd.iota(group_row, [[G, NG]], base=0, channel_multiplier=0).then_inc(S["pool_c"], 1)
            pool.wait_ge(S["pool_c"], 7)
            pool.sem_inc(S["pads_made"], 2)
            nc.gpsimd.memset(pad16[:], NODST).then_inc(S["iotas"], 1)
            pool.wait_ge(S["edges_in"], 32)
            nc.gpsimd.tensor_scalar(tmp_hi, srcs, 0.5, 1.0 / P, ALU.add, ALU.mult).then_inc(S["pool_c"], 1)
            pool.wait_ge(S["pool_c"], 8)
            nc.gpsimd.tensor_scalar(tmp_hi, tmp_hi, -0.5, None, ALU.add).then_inc(S["pool_c"], 1)
            pool.wait_ge(S["pool_c"], 9)
            nc.gpsimd.tensor_scalar(tmp_hi, tmp_hi, MAGIC, None, ALU.add).then_inc(S["pool_c"], 1)
            pool.wait_ge(S["pool_c"], 10)
            nc.gpsimd.tensor_scalar(tmp_hi, tmp_hi, -MAGIC, None, ALU.add).then_inc(S["pool_c"], 1)
            pool.wait_ge(S["pool_c"], 11)
            pool.sem_inc(S["lohi"], 1)
            pool.wait_ge(S["chunk_at"], 1)
            for j in range(NG // P):
                nc.gpsimd.indirect_dma_start(found[:, j, :], None, dst.rearrange("(a b) -> a b", b=1),
                                             bass.IndirectOffsetOnAxis(gs_i[:, 0, j:j + 1], 0)).then_inc(S["chunk_in"], 16)
            pool.wait_ge(S["gst_made"], 1)
            pool.wait_ge(S["key_out"], 32)
            pool.wait_ge(S["dst16_out"], 32)
            for j in range(NG // P):
                nc.gpsimd.indirect_dma_start(wedge[j].rearrange("p e c -> p (e c)"), None, keyd,
                                             bass.IndirectOffsetOnAxis(gs_i[:, 1, j:j + 1], 0)).then_inc(S["wedge_in"], 16)
            pool.wait_ge(S["lohi"], 3)
            for h in range(2):
                pool.wait_ge(S[f"pre_tab{h}"], 16 + 16 * XH)
            pool.wait_ge(S["keyT"], NG // P)
            pool.wait_ge(S["windows_made"], 1)
            R, RD, RG, G1 = rounds(pool)

            def gather(r, table, k0):
                with pool.Fori(0, XH) as p:
                    k = k0 + p
                    for h in range(2):
                        pool.wait_ge(S[f"edge_in{h}"], 16 * (k + 1))
                        for c in range(2):
                            pool.wait_ge(S[f"used{h}{c}"], UP + k)
                            settle(pool)
                            for t in range(c * TC, (c + 1) * TC):
                                nc.gpsimd.indirect_dma_start(
                                    rows[h][:, t, :], None, table,
                                    bass.IndirectOffsetOnAxis(edge[h][:, t, 0:1].bitcast(u32), 0)) \
                                    .then_inc(S[f"got{h}{c}"], 16)

            with pool.Fori(0, R) as r:
                gather(r, tab0, r * XH)
            with pool.If(G1 > 0), pool.Fori(0, RG) as r:
                pool.wait_ge(S["rs_out"], 16)
                gather(r, tab1, r * XH + R * XH)

        @block.vector
        def _(dve):
            V = nc.vector
            made = [0, 0]

            def own(ins):
                made[0] += 1
                ins.then_inc(S["dve_c"], 1)
                dve.wait_ge(S["dve_c"], made[1] + made[0])

            dve.wait_ge(S["edges_in"], 32)
            own(V.tensor_copy(pairs[:, :, 1:2].bitcast(f32), dsts.unsqueeze(2)))
            V.tensor_copy(spl_s[:], pairs[:, 0:EC:SPL, 1:2].bitcast(f32).rearrange("p e c -> p (e c)")).then_inc(S["split_made"], 1)
            V.tensor_copy(pairs[:, :, 0:1], srcs.unsqueeze(2)).then_inc(S["pairs_made"], 1)
            dve.wait_ge(S["iotas"], 18)
            V.tensor_copy(d16, dsts).then_inc(S["split_made"], 1)
            own(V.tensor_copy(node[:], node_i[:]))
            own(V.tensor_copy(slot[:], slot_i[:]))
            own(V.tensor_copy(slot_b[:], slot_i[:]))
            own(V.tensor_copy(part[:], part_i[:]))
            own(V.tensor_copy(base[:], base_i[:]))
            own(V.tensor_scalar(base_s[:], base[:], SCALE, None, ALU.mult))
            own(V.tensor_scalar(ident_b[:], slot_b[0:P, 0:P], part[0:P, 0:1], None, ALU.is_equal))
            own(V.tensor_copy(rstep[:], rstep_i[:]))
            V.tensor_scalar(ident[:], slot[:], part[:, 0:1], None, ALU.is_equal).then_inc(S["dve_iota"], 1)
            own(V.tensor_copy(iota_kb[:], iota_ki[:]))
            own(V.tensor_copy(thc[:], thc_i[:]))
            own(V.tensor_scalar(gneg[:], thc[:], -float(NB), None, ALU.mult))
            dve.wait_ge(S["pads_made"], 1)
            for c in range(NSP):
                V.tensor_scalar(below[c], group_row, spl_s[:, c:c + 1], None, ALU.is_gt).then_inc(S["compared"], 1)
            dve.wait_ge(S["counted"], 1)
            own(V.tensor_scalar(gs[:, 0, :], ps_m[0:P, 0:NG // P], -1.0, 0.0, ALU.add, ALU.max))
            own(V.tensor_scalar(gs[:, 1, :], gs[:, 0, :], float(SPL), None, ALU.mult))
            V.tensor_copy(gs_i[:, 0, :], gs[:, 1, :]).then_inc(S["chunk_at"], 1)
            dve.wait_ge(S["lohi"], 1)
            V.scalar_tensor_tensor(out=key_pairs[:, :, 1:2], in0=dsts.unsqueeze(2), scalar=float(NB),
                                   in1=tmp_hi.unsqueeze(2), op0=ALU.mult, op1=ALU.add).then_inc(S["lohi"], 1)
            own(V.scalar_tensor_tensor(out=key_pairs[:, :, 0:1], in0=tmp_hi.unsqueeze(2), scalar=-float(P),
                                       in1=srcs.unsqueeze(2), op0=ALU.mult, op1=ALU.add))
            dve.sem_inc(S["lohi"], 1)
            for h in range(2):
                dve.wait_ge(S[f"x_in{h}"], 16)
                for t in range(XH):
                    last = V.bn_stats(stats[:, h * XH + t, :], xs[h][:, t, :])
                own(last)
            for t in range(NB):
                last = V.bn_aggr(mv[:, t, :], stats[:, t, :])
            own(last)
            own(V.tensor_scalar(nmr[:].unsqueeze(2), mv[:, :, 1:2], 1e-5, None, ALU.add))
            V.tensor_scalar(nmr[:], nmr[:], 1.0, None, ALU.mult).then_inc(S["pre_std"], 1)
            dve.wait_ge(S["pre_rstd"], 1)
            own(V.reciprocal(rstd[:], rstd[:]))
            own(V.tensor_tensor(nmr[:].unsqueeze(2), mv[:, :, 0:1], rstd[:].unsqueeze(2), ALU.mult))
            V.tensor_scalar(nmr[:], nmr[:], -1.0, None, ALU.mult).then_inc(S["pre_scaled"], 1)
            dve.wait_ge(S["chunk_in"], 16 * (NG // P))
            own(V.tensor_tensor(found_f, found, over_slots(thc[:], NG // P, SPL), ALU.is_lt))
            own(V.tensor_reduce(gs[:, 2, :], found_f, AX.X, ALU.add))
            V.tensor_tensor(gs[:, 4, :], gs[:, 2, :], gs[:, 1, :], ALU.add).then_inc(S["start_made"], 1)
            dve.wait_ge(S["start_made"], 1)
            V.tensor_copy(gs_i[:, 1, :], gs[:, 4, :]).then_inc(S["gst_made"], 1)
            own(V.memset(st_row[:, NG:NG + 1], float(E)))
            dve.wait_ge(S["start_in"], 16)
            dve.wait_ge(S["pairs_out"], 32)
            own(V.tensor_tensor(win.rearrange("p (r b) -> p r b", b=NB),
                                over_tiles(st_row[:, 0:NG:GB], RMAX, NB),
                                over_slots(rstep[:, 0:RMAX], RMAX, NB), ALU.add))
            own(V.tensor_scalar(win, win, float(E), None, ALU.min))
            own(V.tensor_tensor(gap[:], st_row[:, GB:NG + 1:GB], st_row[:, 0:NG:GB], ALU.subtract))
            own(V.tensor_reduce(rnd_f[:, 0:1], gap[:], AX.X, ALU.max))
            own(V.tensor_scalar(rnd_f[:, 2:2 + RMAX], rstep[:, 0:RMAX], rnd_f[:, 0:1], None, ALU.is_lt))
            own(V.tensor_reduce(rnd_f[:, 1:2], rnd_f[:, 2:2 + RMAX], AX.X, ALU.add))
            own(V.tensor_scalar(flags[:, 0:1], rnd_f[:, 1:2], 1.0, None, ALU.max))
            own(V.tensor_tensor(steps_row, st_row[:, 1:NG + 1], st_row[:, 0:NG], ALU.subtract))
            own(V.tensor_reduce(flags[:, 4:5], steps_row, AX.X, ALU.max))
            own(V.tensor_scalar(flags[:, 5:6], flags[:, 4:5], float(WG), None, ALU.is_le))
            own(V.tensor_scalar(flags[:, 6:7], flags[:, 0:1], 1.0, None, ALU.is_le))
            own(V.tensor_tensor(flags[:, 1:2], flags[:, 5:6], flags[:, 6:7], ALU.mult))
            own(V.tensor_scalar(flags[:, 3:4], flags[:, 1:2], -1.0, 1.0, ALU.mult, ALU.add))
            own(V.tensor_tensor(flags[:, 2:3], flags[:, 0:1], flags[:, 3:4], ALU.mult))
            V.tensor_copy(rnd[:], flags[:, 0:4]).then_inc(S["windows_made"], 1)
            dve.wait_ge(S["wedge_in"], 16 * (NG // P))
            for j in range(NG // P + 1):
                h = j % 2
                if j < NG // P:
                    if j >= 2:
                        dve.wait_ge(S["keyT"], j - 1)
                    own(V.tensor_scalar(xt[h][:].unsqueeze(2), wedge[j][:, :, 1:2], gneg[:, j:j + 1], -1.0,
                                        ALU.add, ALU.max))
                    own(V.tensor_scalar(xt[h][:], xt[h][:], float(KEYS), None, ALU.min))
                    dve.sem_inc(S["key_made"], 1)
                if j:
                    dve.wait_ge(S["keyT"], j)
                    V.tensor_copy(keys[:, :, (j - 1) * P:j * P], ps_key[1 - h]).then_inc(S["keys_made"], 1)
            dve.wait_ge(S["consts_in"], 9 * 16)
            made[1], start = made[0], made[0]
            made[0] = 0
            n_own = 4
            with dve.Fori(0, XH) as p:
                for h in range(2):
                    made[0] = 0
                    made[1] = start + (2 * p + h) * n_own
                    t = 2 * p + h
                    dve.wait_ge(S["h_ps"], t + 1)
                    dve.wait_ge(S[f"pre_tab{h}"], 16 + 16 * p)
                    own(V.tensor_tensor(trow[h][:, 0:D], ps_a[h][0:P, 0:D], bv_s[:], ALU.add))
                    own(V.tensor_tensor_reduce(out=junk[:], in0=trow[h][:, 0:D], in1=wq_s[:], scale=1.0, scalar=0.0,
                                               op0=ALU.mult, op1=ALU.add, accum_out=sm[:, 0:1]))
                    own(V.tensor_tensor_reduce(out=junk[:], in0=trow[h][:, 0:D], in1=wk_s[:], scale=1.0, scalar=0.0,
                                               op0=ALU.mult, op1=ALU.add, accum_out=sm[:, 1:2]))
                    V.tensor_scalar(trow[h][:, QC:QC + 1], sm[:, 0:1], bqk[:, 0:1], None, ALU.add).then_inc(S["h_row"], 1)
                    own(V.tensor_scalar(kcol[:, bass.ds(t, 1)], sm[:, 1:2], bqk[:, 1:2], None, ALU.add))
                    assert made[0] == n_own
            made[0], made[1] = 0, start + NB * n_own
            dve.wait_ge(S["h_row"], UP + NB)
            own(V.tensor_copy(k3[:, :, 0], kcol[:]))
            own(V.tensor_tensor(k_rest[:], kcol[:], k3[:, :, 0], ALU.subtract))
            own(V.tensor_copy(k3[:, :, 1], k_rest[:]))
            own(V.tensor_tensor(k_rest[:], k_rest[:], k3[:, :, 1], ALU.subtract))
            V.tensor_copy(k3[:, :, 2], k_rest[:]).then_inc(S["k3_made"], 1)
            R, RD, RG, G1 = rounds(dve)
            start += NB * n_own + 4
            n_own, n_fin = 47, 7
            dve.wait_ge(S["keys_made"], NG // P)
            finished = [0, 0]

            def own_f(ins):
                finished[0] += 1
                ins.then_inc(S["dve_f"], 1)
                dve.wait_ge(S["dve_f"], finished[1] + finished[0])

            def near(b, k, h):
                dve.wait_ge(S[f"edge_in{h}"], 16 * (k + 1))
                V.tensor_scalar(ndl[h][:].unsqueeze(2), edge[h][:, :, 1:2].bitcast(f32), -SCALE,
                                base_s[:, bass.ds(b, 1)], ALU.mult, ALU.add).then_inc(S[f"ndl_made{h}"], 1)

            def look_up(b, k, h):
                dve.wait_ge(S["dT_in"], 16 * (2 * k + h + 1))
                V.tensor_scalar(dT[:].bitcast(bf16), dT[:], node[:, bass.ds(b, 1)], None, ALU.is_equal) \
                    .then_inc(S["ohT_made"], 1)

            def one_hots(i, b, c):
                n, at0 = NC * i + c, SLOTS[c] * GC * 2
                dve.wait_ge(S["ring_used"], n + (2, 2, -1, 1, 1)[c])
                V.tensor_tensor(oh_low[:, at0 * P:(at0 + 2 * GC) * P].rearrange("p (g a s) -> p g a s", a=2, s=P),
                                slot_b[:, 0:P].unsqueeze(1).unsqueeze(1).to_broadcast([128, GC, 2, P]),
                                keys[:, 0:2, bass.ds(b * GB + c * GC, GC)].rearrange("p a g -> p g a").unsqueeze(3)
                                .to_broadcast([128, GC, 2, P]), ALU.is_equal)
                for g in range(GC):
                    for half in range(2):
                        at = at0 + 2 * g + half
                        last = V.tensor_scalar(oh_key[:, at * KEYS:(at + 1) * KEYS], iota_kb[:],
                                               kb[:, half, c * GC + g:c * GC + g + 1], None, ALU.is_equal)
                last.then_inc(S["ring_full"], 1)

            def weigh(b, k, h, behind):
                i, col = 2 * k + h, bass.ds(b, 1)
                made[0], made[1] = 0, start + i * n_own
                w, e = wts[h], ew[h]
                q = rows[h][:, :, QC:QC + 1].rearrange("p t c -> p (t c)")
                dve.wait_ge(S[f"sq_made{h}"], k + 1)
                for t in range(T):
                    if t % TC == 0:
                        dve.wait_ge(S[f"got{h}{t // TC}"], TC * 16 * (k + 1))
                    q_t = rows[h][:, t, QC:QC + 1]
                    if t < 2:
                        ins = V.tensor_scalar(qm[:, t, :], w[:, t, 0:P], q_t, None, ALU.subtract)
                    else:
                        ins = V.scalar_tensor_tensor(out=qm[:, t % 2, :], in0=w[:, t, :], scalar=q_t,
                                                     in1=qm[:, t % 2, :], op0=ALU.subtract, op1=ALU.min)
                    made[0] += 1
                    ins.then_inc(S["dve_c"], 1)
                    dve.wait_ge(S["dve_c"], made[1] + made[0] - (t < T - 1))
                V.tensor_tensor(qm[:, 2, :], qm[:, 0, :], qm[:, 1, :], ALU.min).then_inc(S["half_max"], 1)
                dve.wait_ge(S["ke_made"], i + 1)
                own(V.tensor_reduce(e[:, 0, :], ps_k[:, 0:3 * T].rearrange("p (t c) -> p t c", c=3), AX.X, ALU.add))
                own(V.tensor_tensor(e[:, 1, :], e[:, 0, :], q, ALU.add))
                own(V.scalar_tensor_tensor(out=e[:, 2, :], in0=e[:, 1, :], scalar=0.2, in1=e[:, 1, :],
                                           op0=ALU.mult, op1=ALU.max))
                dve.wait_ge(S["qT_made"], i + 1)
                own(V.tensor_reduce(sc[:, 0:1], ps_q[0:P, 0:128], AX.X, ALU.min))
                own(V.scalar_tensor_tensor(out=sc[:, 1:2], in0=sc[:, 0:1], scalar=-1.0, in1=kcol[:, col],
                                           op0=ALU.mult, op1=ALU.add))
                own(V.scalar_tensor_tensor(out=sc[:, 2:3], in0=sc[:, 1:2], scalar=0.2, in1=sc[:, 1:2],
                                           op0=ALU.mult, op1=ALU.max))
                own(V.tensor_tensor(sc[:, 3:4], sc[:, 2:3], mcol[:, col], ALU.max))
                own(V.tensor_copy(m3[:, 0:1], sc[:, 3:4]))
                own(V.tensor_tensor(sc[:, 4:5], sc[:, 3:4], m3[:, 0:1], ALU.subtract))
                own(V.tensor_copy(m3[:, 1:2], sc[:, 4:5]))
                own(V.tensor_tensor(sc[:, 5:6], sc[:, 4:5], m3[:, 1:2], ALU.subtract))
                V.tensor_copy(m3[:, 2:3], sc[:, 5:6]).then_inc(S["m3_made"], 1)
                V.tensor_tensor(corr[h][:, 0:1], mcol[:, col], sc[:, 3:4], ALU.subtract).then_inc(S["corr_in"], 1)
                dve.wait_ge(S["corr_in"], i + 1)
                own(V.tensor_tensor(mcol[:, col], sc[:, 3:4], sc[:, 3:4], ALU.max))
                if behind:
                    finish(*behind)
                dve.wait_ge(S["ring_full"], UP + NC * i)
                own(V.tensor_scalar(kb[:], keys[:, 2:4, bass.ds(b * GB, GB)], 0.0, None, ALU.add))
                one_hots(i, b, 0)
                one_hots(i, b, 1)
                dve.wait_ge(S["me_made"], UP + i + 1)
                V.tensor_reduce(e[:, 4, :], ps_m[:, 0:3 * T].rearrange("p (t c) -> p t c", c=3), AX.X, ALU.add) \
                    .then_inc(S["w_read"], 1)
                dve.wait_ge(S["w_read"], i + 1)
                V.tensor_tensor(e[:, 5, :], e[:, 2, :], e[:, 4, :], ALU.subtract).then_inc(S["lw_made"], 1)
                assert made[0] == n_own, made[0]

            def finish(b, k, h):
                i, col = 2 * k + h, bass.ds(b, 1)
                finished[0], finished[1] = 0, i * n_fin
                dve.wait_ge(S["corr_made"], i + 1)
                dve.wait_ge(S[f"used{h}1"], UP + k + 1)
                dve.wait_ge(S[f"acc_in{h}"], 16 * (k + 1))
                dve.wait_ge(S[f"acc_out{h}"], 16 + 16 * k)
                V.scalar_tensor_tensor(out=acc_new[h][:], in0=acc_old[h][:], scalar=corr[h][:, 1:2],
                                       in1=ps_a[h][0:P, 0:D + 1], op0=ALU.mult, op1=ALU.add) \
                    .then_inc(S[f"acc_made{h}"], 1)
                dve.wait_ge(S[f"acc_made{h}"], UP + k + 1)
                own_f(V.tensor_scalar(sf[:, 0:1], acc_new[h][:, D:D + 1], 1e-30, None, ALU.max))
                own_f(V.tensor_scalar(filled[:, col], acc_new[h][:, D:D + 1], 0.0, None, ALU.is_gt))
                own_f(V.reciprocal(sf[:, 1:2], sf[:, 0:1]))
                dve.wait_ge(S[f"x_in_l{h}"], 16 * (k + 1))
                dve.wait_ge(S[f"x1_out{h}"], 16 + 16 * k)
                own_f(V.scalar_tensor_tensor(out=x1t[h][:], in0=acc_new[h][:, 0:D], scalar=sf[:, 1:2],
                                             in1=xt[h][:], op0=ALU.mult, op1=ALU.add))
                dve.sem_inc(S[f"x1_made{h}"], 1)
                own_f(V.bn_stats(stats[:, 0, :], x1t[h][:]))
                settle(dve)
                own_f(V.bn_aggr(sf[:, 4:6], stats[:, 0, :]))
                own_f(V.tensor_scalar(mv[:, col, :].rearrange("p a c -> p (a c)"), sf[:, 4:6], 0.0, None, ALU.add))
                assert finished[0] == n_fin, finished[0]

            def step(b, k, h, ahead, after, behind):
                weigh(b, k, h, behind)
                one_hots(2 * k + h, b, 2)
                if ahead:
                    look_up(*ahead)
                for c in range(3, NC):
                    one_hots(2 * k + h, b, c)
                if after:
                    near(*after)

            with dve.Fori(0, R) as r:
                near(0, r * XH, 0)
                near(1, r * XH, 1)
                look_up(0, r * XH, 0)
                step(0, r * XH, 0, (1, r * XH, 1), (2, r * XH + 1, 0), None)
                with dve.Fori(0, XH - 2) as p:
                    k = r * XH + p
                    step(2 * p + 1, k, 1, (2 * p + 2, k + 1, 0), (2 * p + 3, k + 1, 1), (2 * p, k, 0))
                    step(2 * p + 2, k + 1, 0, (2 * p + 3, k + 1, 1), (2 * p + 4, k + 2, 0), (2 * p + 1, k, 1))
                k = r * XH + XH - 1
                step(NB - 3, k - 1, 1, (NB - 2, k, 0), (NB - 1, k, 1), (NB - 4, k - 1, 0))
                step(NB - 2, k, 0, (NB - 1, k, 1), None, (NB - 3, k - 1, 1))
                step(NB - 1, k, 1, None, None, (NB - 2, k, 0))
                finish(NB - 1, k, 1)
            dve.wait_ge(S["deg_ps"], R)
            V.tensor_reduce(outdeg[:], ps_h[0:P, 0:HC].rearrange("p (s u) -> p u s", u=NB), AX.X, ALU.add) \
                .then_inc(S["deg_read"], 1)
            steps0 = R * NB
            start0 = start + steps0 * n_own
            made[0], made[1] = 0, start0
            with dve.If(G1 > 0):
                dve.wait_ge(S["deg_read"], 1)
                settle(dve)
                dve.wait_ge(S["g_src_in"], 16)

                def own_g(ins, n):
                    ins.then_inc(S["dve_g"], 1)
                    dve.wait_ge(S["dve_g"], n)

                own_g(V.tensor_scalar(g_hi, g_src, 0.5, 1.0 / P, ALU.add, ALU.mult), 1)
                own_g(V.tensor_scalar(g_hi, g_hi, -0.5, None, ALU.add), 2)
                own_g(V.tensor_scalar(g_hi, g_hi, MAGIC, None, ALU.add), 3)
                own_g(V.tensor_scalar(g_hi, g_hi, -MAGIC, None, ALU.add), 4)
                own_g(V.scalar_tensor_tensor(out=g_lo, in0=g_hi, scalar=-float(P), in1=g_src,
                                             op0=ALU.mult, op1=ALU.add), 5)
                own_g(V.memset(outdeg[:], 0.0), 6)
                with dve.Fori(0, NB) as b:
                    cols = bass.ds(b * HT, HT)
                    dve.wait_ge(S["hist_made"], UP + b)
                    V.tensor_tensor(oh_lo, over_tiles(slot_b[0:P, 0:P], HT, P),
                                    over_slots(g_lo[:, cols], HT, P), ALU.is_equal).then_inc(S["oh_made"], 1)
                    V.tensor_tensor(oh_hi, over_tiles(slot_b[0:P, 0:NB], HT, NB),
                                    over_slots(g_hi[:, cols], HT, NB), ALU.is_equal).then_inc(S["oh_made"], 1)
                    dve.wait_ge(S["hist_ps"], UP + b + 1)
                    V.tensor_tensor(outdeg[:], ps_h[0:P, 0:NB], outdeg[:], ALU.add).then_inc(S["hist_made"], 1)
                dve.wait_ge(S["hist_made"], UP + NB)
            dve.wait_ge(S["deg_read"], 1)
            V.tensor_scalar(outdeg[:], outdeg[:], 1.0, None, ALU.max).then_inc(S["deg_made"], 1)
            dve.wait_ge(S["dve_f"], R * NB * n_fin)
            settle(dve)
            V.tensor_scalar(nmr[:].unsqueeze(2), mv[:, :, 1:2], 1e-5, None, ALU.add).then_inc(S["deg_made"], 1)
            dve.wait_ge(S["sod_made"], 2)
            V.reciprocal(rso[:], sod[:]).then_inc(S["rs_made"], 1)
            V.reciprocal(rstd1[:], rstd[:]).then_inc(S["rs_made"], 1)
            dve.wait_ge(S["rs_made"], 2)
            V.scalar_tensor_tensor(out=nmr1[:].unsqueeze(2), in0=mv[:, :, 0:1], scalar=-1.0, in1=rstd1[:].unsqueeze(2),
                                   op0=ALU.mult, op1=ALU.mult).then_inc(S["rs_made"], 1)
            dve.wait_ge(S["rs_made"], 3)
            V.tensor_tensor(rstd[:], rstd1[:], rso[:], ALU.mult).then_inc(S["rs_made"], 1)
            V.tensor_tensor(nmr[:], nmr1[:], rso[:], ALU.mult).then_inc(S["rs_made"], 1)
            n_pre = made[0]

            def emit(i, j, h, b):
                dve.wait_ge(S["o_ps"], i + 1)
                dve.wait_ge(S[f"y_out{h}"], 16 + 16 * j)
                own(V.scalar_tensor_tensor(out=y[h][:], in0=ps_o[0:P, 0:D], scalar=filled[:, bass.ds(b, 1)],
                                           in1=b1_s[:], op0=ALU.mult, op1=ALU.add))
                dve.sem_inc(S["o_read"], 1)
                own(V.scalar_tensor_tensor(out=y[h][:], in0=y[h][:], scalar=0.01, in1=y[h][:],
                                           op0=ALU.mult, op1=ALU.max))
                V.tensor_tensor_reduce(out=junk[:], in0=y[h][:], in1=y[h][:], scale=1.0, scalar=0.0,
                                       op0=ALU.mult, op1=ALU.add, accum_out=sm[:, 0:1]).then_inc(S["ss_made"], 1)
                dve.wait_ge(S["norm_made"], i + 1)
                own(V.tensor_scalar(sm[:, 1:2], sm[:, 2:3], 1e-12, None, ALU.max))
                own(V.reciprocal(sm[:, 3:4], sm[:, 1:2]))
                dve.wait_ge(S[f"x1_in{h}"], 16 * (j + 1))
                own(V.scalar_tensor_tensor(out=y[h][:], in0=y[h][:], scalar=sm[:, 3:4], in1=xt[h][:],
                                           op0=ALU.mult, op1=ALU.add))
                dve.sem_inc(S[f"y_made{h}"], 1)

            with dve.If(RD > 0):
                with dve.Fori(0, NB // FG // 2) as g:
                    for h in range(2):
                        n = 2 * g + h
                        dve.wait_ge(S["a_made"], n + 1)
                        dve.wait_ge(S["c_made"], n + 1)
                        V.tensor_tensor(rest[h], f_in[h], split[:, bass.ds(n * FG, FG), 0:D], ALU.subtract) \
                            .then_inc(S["r_made"], 1)
                        dve.wait_ge(S["r_made"], n + 1)
                        dve.sem_inc(S["fin_used"], 1)
                        dve.wait_ge(S["b_made"], UP + n + 1)
                        V.tensor_tensor(split[:, bass.ds(n * FG, FG), 2 * D:3 * D], rest[h],
                                        split[:, bass.ds(n * FG, FG), D:2 * D], ALU.subtract).then_inc(S["c_made"], 1)

                def combine(p, h):
                    col = bass.ds(2 * p + h, 1)
                    dve.wait_ge(S[f"d_sum{h}"], UP + p + 1)
                    dve.wait_ge(S[f"f2_made{h}"], p + 1)
                    V.scalar_tensor_tensor(out=U[h][:], in0=ps_a[h][0:P, 0:D], scalar=rso[:, col], in1=F[h][:],
                                           op0=ALU.mult, op1=ALU.add).then_inc(S["up_made"], 1)
                    V.scalar_tensor_tensor(out=F[h][:], in0=ps_a[h][0:P, 0:D], scalar=rso[:, col], in1=F[h][:],
                                           op0=ALU.mult, op1=ALU.mult).then_inc(S["up_made"], 1)

                def embed(p, h):
                    i = 2 * p + h
                    made[0], made[1] = 0, start0 + n_pre + i * 5
                    emit(i, p, h, i)
                    assert made[0] == 5, made[0]

                combine(0, 0)
                with dve.Fori(0, XH - 1) as p:
                    combine(p, 1)
                    embed(p, 0)
                    combine(p + 1, 0)
                    embed(p, 1)
                combine(XH - 1, 1)
                embed(XH - 1, 0)
                embed(XH - 1, 1)
            n_own = 7
            with dve.If(G1 > 0), dve.Fori(0, RG) as r:
                with dve.Fori(0, XH) as p:
                    j = r * XH + p
                    k = j + R * XH
                    for h in range(2):
                        i, b = 2 * j + h, 2 * p + h
                        col = bass.ds(b, 1)
                        made[0], made[1] = 0, start0 + n_pre + i * n_own
                        w = wts[h]
                        dve.wait_ge(S[f"edge_in{h}"], 16 * (k + 1))
                        made[0] += 1
                        V.tensor_scalar(ndl[h][:].unsqueeze(2), edge[h][:, :, 1:2].bitcast(f32), base[:, col], None,
                                        ALU.subtract).then_inc(S["dve_c"], 1)
                        dve.wait_ge(S["dve_c"], made[1] + made[0])
                        dve.sem_inc(S[f"ndl_made{h}"], 1)
                        dve.wait_ge(S[f"used{h}1"], UP + k)
                        own(V.tensor_tensor(w[:], over_tiles(slot[:, 0:P], T, P), over_slots(ndl[h][:], T, P), ALU.is_equal))
                        for c in range(2):
                            part_ = w[:, c * TC:(c + 1) * TC, :]
                            dve.wait_ge(S[f"got{h}{c}"], TC * 16 * (k + 1))
                            V.tensor_tensor(part_, part_,
                                            rows[h][:, c * TC:(c + 1) * TC, RS:RS + 1].to_broadcast([128, TC, P]),
                                            ALU.mult).then_inc(S[f"w_made{h}{c}"], 1)
                        dve.wait_ge(S[f"used{h}1"], UP + k + 1)
                        av = acc_new[h][:, 0:D]
                        dve.wait_ge(S[f"acc_in{h}"], 16 * (k + 1))
                        dve.wait_ge(S[f"acc_out{h}"], 16 + 16 * k)
                        V.scalar_tensor_tensor(out=av, in0=acc_old[h][:, 0:D], scalar=later[0:P, bass.ds(r, 1)],
                                               in1=ps_a[h][0:P, 0:D], op0=ALU.mult, op1=ALU.add) \
                            .then_inc(S[f"acc_made{h}"], 1)
                        dve.wait_ge(S[f"acc_made{h}"], UP + k + 1)
                        dve.wait_ge(S[f"f2_made{h}"], j + 1)
                        V.scalar_tensor_tensor(out=U[h][:], in0=av, scalar=rso[:, col], in1=F[h][:],
                                               op0=ALU.mult, op1=ALU.add).then_inc(S["up_made"], 1)
                        V.scalar_tensor_tensor(out=F[h][:], in0=av, scalar=rso[:, col], in1=F[h][:],
                                               op0=ALU.mult, op1=ALU.mult).then_inc(S["up_made"], 1)
                        emit(i, j, h, b)
                        assert made[0] == n_own, made[0]

        @block.scalar
        def _(act):
            A = nc.scalar
            for w_s, w_d in ((Wv_s, Wv), (W1_s, W1), (W2_s, W2)):
                act.dma_start(w_s[:], w_d.rearrange("(c p) n -> p c n", p=128)).then_inc(S["consts_in"], 16)
            for r_s, r_d in ((bv_s, bv), (wq_s, wq), (wk_s, wk), (b1_s, b1)):
                act.dma_start(r_s[:], r_d.unsqueeze(0).to_broadcast([P, D])).then_inc(S["consts_in"], 16)
            for c, s_d in enumerate((bq, bk)):
                act.dma_start(bqk[:, c:c + 1], s_d.unsqueeze(0).to_broadcast([P, 1])).then_inc(S["consts_in"], 16)
            for n, name in enumerate(stores):
                act.dma_start(primed[:, n:n + 1], bq.unsqueeze(0)).then_inc(S[name], 16)
            act.wait_ge(S["pre_std"], 1)
            A.activation(rstd[:], nmr[:], ACT.Sqrt).then_inc(S["pre_rstd"], 1)
            act.wait_ge(S["pre_scaled"], 1)
            def normalized(t):
                if t >= 2:
                    act.wait_ge(S["hn_T"], t - 1)
                A.activation(hn[t % 2][:], xs[t // XH][:, t % XH, :], ACT.Relu, bias=nmr[:, t:t + 1],
                             scale=rstd[:, t:t + 1]).then_inc(S["hn_made"], 1)

            normalized(0)
            for t in range(NB):
                if t + 1 < NB:
                    normalized(t + 1)
                act.wait_ge(S["hn_T"], t + 1)
                if t >= 2:
                    act.wait_ge(S["h_ps"], t - 1)
                A.activation(hT[t % 2][:, 0:2, :], ps_tt[t % 2][:, 0:2, 0:P], ACT.Copy).then_inc(S["hT_made"], 1)
            act.wait_ge(S["windows_out"], 16)
            R, RD, RG, G1 = rounds(act)

            def distances(b, k, h, c):
                act.wait_ge(S[f"ndl_made{h}"], UP + k + 1)
                act.wait_ge(S[f"used{h}{c}"], UP + k)
                for t in range(c * TC, (c + 1) * TC):
                    last = A.activation(wts[h][:, t, :], slot[:, 0:P], ACT.Square, bias=ndl[h][:, t:t + 1], scale=SCALE)
                if c == 1:
                    last.then_inc(S[f"sq_made{h}"], 1)

            def copy_counts(i, h, c):
                for u in range(3):
                    v, g = 3 * (NC * i + c) + u, c * GC + 2 * u
                    width = (2 if u < 2 else 1) * KEYS
                    act.wait_ge(S["ct_ps"], v + 1)
                    if c in (0, 2) and u == 0:
                        act.wait_ge(S["deg_part"], 1 + 2 * i + c // 2)
                        settle(act)
                        act.wait_ge(S[f"ct_out{c // 2}"], 16 + 16 * i)
                    A.activation(count[:, g * KEYS:g * KEYS + width], ps_ct[v_bank(h, c, u)][:, 0:width], ACT.Copy) \
                        .then_inc(S["ct_copied"], 1)

            def store_counts(b, i, part_):
                c0, c1 = ((0, 2), (2, NC))[part_]
                act.wait_ge(S["ct_copied"], 2 + 3 * (NC * i + c1))
                cols = slice(c0 * GC * KEYS, c1 * GC * KEYS)
                act.dma_start(countd[bass.ds(b, 1), :, cols].rearrange("a p c -> p (a c)"), count[:, cols]) \
                    .then_inc(S[f"ct_out{part_}"], 16)

            def weights(b, k, h):
                i = 2 * k + h
                A.activation(corr[h][:, 1:2], corr[h][:, 0:1], ACT.Exp).then_inc(S["corr_made"], 1)
                act.wait_ge(S["lw_made"], i + 1)
                for t in range(T):
                    last = A.activation(wts[h][:, t, :], wts[h][:, t, :], ACT.Exp, bias=ew[h][:, 5, t:t + 1],
                                        scale=-1.0)
                    if t == TF - 1:
                        last.then_inc(S[f"w_first{h}"], 1)
                    if t % TC == TC - 1:
                        last.then_inc(S[f"w_made{h}{t // TC}"], 1)

            def store_sums(b, k, h):
                rows_of = bass.ds(b * P, P)
                act.wait_ge(S[f"acc_made{h}"], UP + k + 1)
                act.dma_start(accd[rows_of, :], acc_new[h][:]).then_inc(S[f"acc_out{h}"], 16)
                act.wait_ge(S[f"x1_made{h}"], UP + k + 1)
                act.dma_start(x1d[rows_of, :], x1t[h][:]).then_inc(S[f"x1_out{h}"], 16)

            def step(b, k, h, ahead, behind):
                i = 2 * k + h
                copy_counts(i, h, 0)
                copy_counts(i, h, 1)
                store_counts(b, i, 0)
                act.wait_ge(S["corr_in"], i + 1)
                weights(b, k, h)
                if behind:
                    store_sums(*behind)
                if ahead:
                    distances(*ahead, 0)
                for c in range(2, NC):
                    copy_counts(i, h, c)
                store_counts(b, i, 1)
                if ahead:
                    distances(*ahead, 1)

            with act.Fori(0, R) as r:
                for h in range(2):
                    for c in range(2):
                        distances(h, r * XH, h, c)
                step(0, r * XH, 0, (2, r * XH + 1, 0), None)
                with act.Fori(0, XH - 2) as p:
                    k = r * XH + p
                    step(2 * p + 1, k, 1, (2 * p + 3, k + 1, 1), (2 * p, k, 0))
                    step(2 * p + 2, k + 1, 0, (2 * p + 4, k + 2, 0), (2 * p + 1, k, 1))
                k = r * XH + XH - 1
                step(NB - 3, k - 1, 1, (NB - 1, k, 1), (NB - 4, k - 1, 0))
                step(NB - 2, k, 0, None, (NB - 3, k - 1, 1))
                step(NB - 1, k, 1, None, (NB - 2, k, 0))
                store_sums(NB - 1, k, 1)
            act.wait_ge(S["deg_made"], 2)
            A.activation(sod[:], outdeg[:], ACT.Sqrt).then_inc(S["sod_made"], 1)
            A.activation(rstd[:], nmr[:], ACT.Sqrt).then_inc(S["sod_made"], 1)
            act.wait_ge(S["rs_made"], 5)

            def relu(b, j, h):
                act.wait_ge(S[f"x1_in{h}"], 16 * (j + 1))
                A.activation(F[h][:], xt[h][:], ACT.Relu, bias=nmr1[:, bass.ds(b, 1)],
                             scale=rstd1[:, bass.ds(b, 1)]).then_inc(S[f"f2_made{h}"], 1)

            def copy_turned(i, h):
                act.wait_ge(S["upT_made"], UP + i + 1)
                A.activation(hT[h][:], ps_t[:, :, 0:P], ACT.Copy).then_inc(S["upT_copied"], 1)

            def store(i, b, j, h):
                act.wait_ge(S["ss_made"], i + 1)
                A.activation(sm[:, 2:3], sm[:, 0:1], ACT.Sqrt).then_inc(S["norm_made"], 1)
                act.wait_ge(S[f"y_made{h}"], UP + j + 1)
                act.dma_start(out[bass.ds(b * P, P), :], y[h][:]).then_inc(S[f"y_out{h}"], 16)

            with act.If(RD > 0):
                for h in range(2):
                    act.wait_ge(S[f"used{h}1"], UP + R * XH)
                    settle(act)

                def high(g, h):
                    n = 2 * g + h
                    act.wait_ge(S[f"fin{h}"], 16 * (g + 1))
                    for t in range(FG):
                        col = bass.ds(n * FG + t, 1)
                        last = A.activation(f_in[h][:, t, :], f_in[h][:, t, :], ACT.Relu, bias=nmr[:, col], scale=rstd[:, col])
                    last.then_inc(S["v_made"], 1)
                    act.wait_ge(S["v_made"], n + 1)
                    A.activation(split[:, bass.ds(n * FG, FG), 0:D], f_in[h], ACT.Copy).then_inc(S["a_made"], 1)

                def middle(g, h):
                    n = 2 * g + h
                    act.wait_ge(S["r_made"], n + 1)
                    A.activation(split[:, bass.ds(n * FG, FG), D:2 * D], rest[h], ACT.Copy).then_inc(S["b_made"], 1)

                last_g = NB // FG // 2 - 1
                high(0, 0)
                with act.Fori(0, last_g) as g:
                    high(g, 1)
                    middle(g, 0)
                    high(g + 1, 0)
                    middle(g, 1)
                high(last_g, 1)
                middle(last_g, 0)
                middle(last_g, 1)
                relu(0, 0, 0)
                relu(1, 0, 1)
                with act.Fori(0, XH - 1) as p:
                    for h in range(2):
                        i = 2 * p + h
                        copy_turned(i, h)
                        store(i, i, p, h)
                        relu(i + 2, p + 1, h)
                for h in range(2):
                    copy_turned(NB - 2 + h, h)
                    store(NB - 2 + h, NB - 2 + h, XH - 1, h)
            with act.If(G1 > 0), act.Fori(0, XH) as p:
                for h in range(2):
                    b = 2 * p + h
                    act.wait_ge(S[f"g_x1_in{h}"], 16 * (p + 1))
                    act.wait_ge(S[f"f_out{h}"], 16 + 16 * p)
                    A.activation(trow[h][:, 0:D], xt[h][:], ACT.Relu, bias=nmr1[:, bass.ds(b, 1)],
                                 scale=rstd1[:, bass.ds(b, 1)]).then_inc(S[f"f_made{h}"], 1)
                    act.wait_ge(S[f"f_made{h}"], UP + p + 1)
                    act.dma_start(tab1[bass.ds(b * P, P), :], trow[h][:]).then_inc(S[f"f_out{h}"], 16)
            with act.If(G1 > 0), act.Fori(0, RG) as r:
                with act.Fori(0, XH) as p:
                    j = r * XH + p
                    for h in range(2):
                        i, b = 2 * j + h, 2 * p + h
                        act.wait_ge(S["upT_made"], UP + i)
                        relu(b, j, h)
                        copy_turned(i, h)
                        act.wait_ge(S[f"acc_made{h}"], UP + j + R * XH + 1)
                        act.dma_start(accd[bass.ds(b * P, P), :], acc_new[h][:]).then_inc(S[f"acc_out{h}"], 16)
                        store(i, b, j, h)

        @block.tensor
        def _(pe):
            TE = nc.tensor
            for name in counters:
                pe.sem_inc(S[name], UP)
            pe.wait_ge(S["dve_iota"], 1)
            pe.wait_ge(S["consts_in"], 9 * 16)

            pe.wait_ge(S["compared"], NSP)
            pe.wait_ge(S["iotas"], 18)
            for j in range(NG // P):
                for c in range(NSP):
                    last = TE.matmul(ps_m[0:P, j:j + 1], below[c][:, j * P:(j + 1) * P], one_b[:], start=(c == 0), stop=(c == NSP - 1))
            last.then_inc(S["counted"], 1)

            def turn(t, h, before):
                pe.wait_ge(S["hn_made"], t + 1)
                pe.wait_ge(S["hT_made"], before)
                for c in range(2):
                    last = TE.transpose(ps_tt[h][:, c, 0:P], hn[h][:, c * 128:(c + 1) * 128], ident[0:P, 0:P])
                last.then_inc(S["hn_T"], 1)

            def project(t, h, read):
                pe.wait_ge(S["hT_made"], UP + t + 1)
                pe.wait_ge(S["h_row"], read)
                for c in range(2):
                    last = TE.matmul(ps_a[h][0:P, 0:D], hT[h][:, c, :], Wv_s[:, c, :], start=(c == 0), stop=(c == 1))
                last.then_inc(S["h_ps"], 1)

            for j in range(NG // P):
                h = j % 2
                pe.wait_ge(S["key_made"], j + 1)
                if j >= 2:
                    pe.wait_ge(S["keys_made"], j - 1)
                for half in range(2):
                    e0 = half * 128
                    TE.transpose(ps_key[h][:, half, :], wedge[j][:, e0:e0 + 128, 0], ident[0:P, 0:P])
                    last = TE.transpose(ps_key[h][:, 2 + half, :], xt[h][:, e0:e0 + 128], ident[0:P, 0:P])
                last.then_inc(S["keyT"], 1)
            turn(0, 0, UP)
            turn(1, 1, UP)
            project(0, 0, UP)
            with pe.Fori(0, XH - 1) as p:
                turn(2 * p + 2, 0, UP + 2 * p + 1)
                project(2 * p + 1, 1, 2 * p + UP)
                turn(2 * p + 3, 1, UP + 2 * p + 2)
                project(2 * p + 2, 0, 2 * p + 1 + UP)
            project(NB - 1, 1, NB - 2 + UP)
            pe.wait_ge(S["windows_made"], 1)
            pe.wait_ge(S["k3_made"], 1)
            pe.wait_ge(S["keys_made"], NG // P)
            pe.wait_ge(S["h_row"], UP + NB)
            R, RD, RG, G1 = rounds(pe)

            def turn_q(i):
                pe.wait_ge(S["half_max"], i + 1)
                TE.transpose(ps_q[0:P, 0:128], qm[:, 2, :], ident[:]).then_inc(S["qT_made"], 1)

            def sums(h, k, width, c, early, turn=None):
                for t in range(c * TC, (c + 1) * TC):
                    if early and t == 0:
                        pe.wait_ge(S[f"w_first{h}"], UP + k + 1)
                    elif t % TC == (TF if early and c == 0 else 0):
                        pe.wait_ge(S[f"w_made{h}{c}"], UP + k + 1)
                    if turn is not None and t == TT:
                        turn_q(turn)
                    last = TE.matmul(ps_a[h][0:P, 0:width], wts[h][:, t, :], rows[h][:, t, 0:width],
                                     start=(t == 0), stop=(t == T - 1))
                last.then_inc(S[f"used{h}{c}"], 1)

            def count_edges(i, h, c):
                n = NC * i + c
                pe.wait_ge(S["ring_full"], UP + n + 1)
                for g in range(GC):
                    u = g // 2
                    if g % 2 == 0:
                        pe.wait_ge(S["ct_copied"], 3 * n + u + 1)
                    for half in range(2):
                        at = (SLOTS[c] * GC + g) * 2 + half
                        last = TE.matmul(ps_ct[v_bank(h, c, u)][:, g % 2 * KEYS:(g % 2 + 1) * KEYS],
                                         oh_low[:, at * P:(at + 1) * P], oh_key[:, at * KEYS:(at + 1) * KEYS],
                                         start=(half == 0), stop=(half == 1))
                    if g == GC - 1:
                        last.then_inc(S["ring_used"], 1)
                        pe.wait_ge(S["ring_used"], 3 + n + 1)
                        pe.sem_inc(S["ct_ps"], 1)
                    elif g % 2:
                        last.then_inc(S["ct_ps"], 1)

            def sum_counts(i, part_, final=False):
                c0, c1 = ((0, 2), (2, NC))[part_]
                pe.wait_ge(S["ct_copied"], 2 + 3 * (NC * i + c1))
                for at in range(c0 * GC * KEYS, c1 * GC * KEYS, HC):
                    width = min(HC, c1 * GC * KEYS - at)
                    last = TE.matmul(ps_h[0:P, 0:width], ident_b[:], count[:, at:at + width], start=False,
                                     stop=final and at + HC >= c1 * GC * KEYS)
                last.then_inc(S["deg_part"], 1)

            def look_up_k(b, i):
                pe.wait_ge(S["ohT_made"], i + 1)
                for t in range(T):
                    last = TE.matmul(ps_k[:, 3 * t:3 * t + 3], dst_hot[:, t, :], k3[:, bass.ds(b, 1), :]
                                     .rearrange("s a c -> s (a c)"), start=True, stop=True)
                last.then_inc(S["ke_made"], 1)

            def look_up_m(i):
                pe.wait_ge(S["m3_made"], i + 1)
                for t in range(T):
                    last = TE.matmul(ps_m[:, 3 * t:3 * t + 3], dst_hot[:, t, :], m3[:], start=True, stop=True)
                last.then_inc(S["me_made"], 1)

            def step(b, k, h, ahead, final=False):
                i = 2 * k + h
                count_edges(i, h, 0)
                count_edges(i, h, 1)
                if ahead:
                    look_up_k(*ahead)
                sums(h, k, D + 1, 0, True)
                sum_counts(i, 0)
                sums(h, k, D + 1, 1, True, i + 1 if ahead else None)
                if ahead:
                    look_up_m(i + 1)
                for c in range(2, NC):
                    count_edges(i, h, c)
                sum_counts(i, 1, final)

            dst_hot = dT[:].bitcast(bf16).rearrange("s (e t) -> s t e", t=T)
            with pe.Fori(0, R) as r:
                look_up_k(0, r * NB)
                turn_q(r * NB)
                look_up_m(r * NB)
                TE.matmul(ps_h[0:P, 0:HC], zero_b[:], keys[0:P].rearrange("p a g -> p (a g)")[:, 0:HC],
                          start=True, stop=False)
                step(0, r * XH, 0, (1, r * NB + 1))
                with pe.Fori(0, XH - 1) as p:
                    k = r * XH + p
                    step(2 * p + 1, k, 1, (2 * p + 2, 2 * k + 2))
                    step(2 * p + 2, k + 1, 0, (2 * p + 3, 2 * k + 3))
                step(NB - 1, r * XH + XH - 1, 1, None, True)
                pe.wait_ge(S["deg_part"], 2 + 2 * NB * (r + 1))
                pe.sem_inc(S["deg_ps"], 1)
            with pe.If(G1 > 0), pe.Fori(0, NB) as b:
                pe.wait_ge(S["oh_made"], 2 * b + 2)
                pe.wait_ge(S["hist_made"], UP + b)
                for t in range(HT):
                    last = TE.matmul(ps_h[0:P, 0:NB], oh_lo[:, t, :], oh_hi[:, t, :], start=(t == 0), stop=(t == HT - 1))
                last.then_inc(S["hist_ps"], 1)

            def transform(i, h):
                pe.wait_ge(S["up_made"], 2 + 2 * i + 2)
                pe.wait_ge(S["upT_copied"], UP + i)
                for c in range(4):
                    m = (U, F)[c // 2][h]
                    last = TE.transpose(ps_t[:, c, 0:P], m[:, c % 2 * 128:(c % 2 + 1) * 128], ident[0:P, 0:P])
                last.then_inc(S["upT_made"], 1)
                pe.wait_ge(S["upT_copied"], UP + i + 1)
                pe.wait_ge(S["o_read"], UP + i)
                for c in range(4):
                    last = TE.matmul(ps_o[0:P, 0:D], hT[h][:, c, :], (W1_s, W2_s)[c // 2][:, c % 2, :],
                                     start=(c == 0), stop=(c == 3))
                last.then_inc(S["o_ps"], 1)

            def dense(p, h, read):
                pe.wait_ge(S[f"ct_in{h}"], 16 * (p + 1))
                pe.wait_ge(S["up_made"], read)
                for u in range(NB):
                    for c in range(3):
                        last = TE.matmul(ps_a[h][0:P, 0:D], counts[h][:, u, :], split[:, u, c * D:(c + 1) * D],
                                         start=(u == 0 and c == 0), stop=(u == NB - 1 and c == 2))
                last.then_inc(S[f"d_sum{h}"], 1)

            with pe.If(RD > 0):
                pe.wait_ge(S["c_made"], 2 + NB // FG)
                dense(0, 0, 2)
                with pe.Fori(0, XH - 1) as p:
                    dense(p, 1, 2 + 4 * p)
                    transform(2 * p, 0)
                    dense(p + 1, 0, 4 + 4 * p)
                    transform(2 * p + 1, 1)
                dense(XH - 1, 1, 2 + 4 * (XH - 1))
                transform(NB - 2, 0)
                transform(NB - 1, 1)
            with pe.If(G1 > 0), pe.Fori(0, RG) as r:
                with pe.Fori(0, XH) as p:
                    j = r * XH + p
                    k = j + R * XH
                    for h in range(2):
                        for c in range(2):
                            sums(h, k, D, c, False)
                        transform(2 * j + h, h)


_INS = ["x", "src", "dst", "L0_gnn_Wv", "L0_gnn_bv", "L0_gnn_wq", "L0_gnn_bq", "L0_gnn_wk", "L0_gnn_bk",
        "L1_gnn_W1", "L1_gnn_W2", "L1_gnn_b"]


def kernel(**inputs):
    import numpy as _np
    import concourse.bacc as _bacc
    from concourse import mybir as _mybir
    from concourse.bass_utils import run_bass_kernel_spmd as _run

    nc = _bacc.Bacc("TRN2", target_bir_lowering=False, num_devices=1)
    arrays, args = {}, []
    for name in _INS:
        a = _np.ascontiguousarray(inputs[name])
        if a.ndim == 0:
            a = a.reshape(1)
        arrays[f"in_{name}"] = a
        args.append(nc.dram_tensor(f"in_{name}", a.shape, _mybir.dt.from_np(a.dtype), kind="ExternalInput").ap())
    args.append(nc.dram_tensor("out_0", (N, D), _mybir.dt.float32, kind="ExternalOutput").ap())
    gnn(nc, *args)
    r = _run(nc, [arrays], core_ids=[0])
    return r.results[0]["out_0"]
```
